# Optimizing a Trainium2 kernel written in Bass

```python
import numpy as np
import jax
import jax.numpy as jnp

def _softmax(x, axis=-1):
    return jax.nn.softmax(x, axis=axis)

def _gelu(x):
    return jax.nn.gelu(x, approximate=True)

def _silu(x):
    return jax.nn.silu(x)

def _sigmoid(x):
    return jax.nn.sigmoid(x)

def _layernorm(x, axis=-1, eps=1e-05):
    m = jnp.mean(x, axis=axis, keepdims=True)
    v = jnp.var(x, axis=axis, keepdims=True)
    return (x - m) / jnp.sqrt(v + eps)

def _scatter_add(tgt, idx, src, axis=0):
    return tgt.at[idx].add(src)

def _segment_sum(src, seg, n):
    return jax.ops.segment_sum(src, seg, n)
kernel_name = 'mk_cond_seq_d2_seqx_r8_1f9e85'

def setup_inputs(seed: int=0):
    np.random.seed(seed)
    _w = jnp.asarray

    def _rec_inputs():
        import jax
        import jax.numpy as jnp
        _rk = jax.random.key(seed)
        x = -0.0003482 + 1 * jax.random.normal(jax.random.fold_in(_rk, 1), (32, 32, 144), jnp.float32)
        _lenS = 32 - jax.random.randint(jax.random.fold_in(_rk, 7), (32,), 0, max(1, 32 // 4) + 1, jnp.int32)
        _lenS2 = 32 - jax.random.randint(jax.random.fold_in(_rk, 8), (32,), 0, max(1, 32 // 4) + 1, jnp.int32)
        cond_1152 = -0.00342701 + 1.00097 * jax.random.normal(jax.random.fold_in(_rk, 11), (32, 144), jnp.float32)
        return (x, cond_1152)
    x, cond_1152 = _rec_inputs()

    def _L0_cond_setup():
        import jax, jax.numpy as jnp
        import numpy as np
        B, T, D, H = (64, 32, 144, 16)
        HD = D // H
        EPS = 1e-06

        def _ln(x):
            mu = jnp.mean(x, axis=-1, keepdims=True)
            var = jnp.var(x, axis=-1, keepdims=True)
            return (x - mu) * jax.lax.rsqrt(var + EPS)

        def _modulate(x, shift, scale):
            return x * (1.0 + scale[:, None, :]) + shift[:, None, :]

        def _attn(x, Wq, Wk, Wv, Wp, bp):
            b, t, d = x.shape
            q = (x @ Wq).reshape(b, t, H, HD).transpose(0, 2, 1, 3)
            k = (x @ Wk).reshape(b, t, H, HD).transpose(0, 2, 1, 3)
            v = (x @ Wv).reshape(b, t, H, HD).transpose(0, 2, 1, 3)
            scores = jnp.einsum('bhqd,bhkd->bhqk', q, k) / np.sqrt(HD)
            mask = jnp.triu(jnp.ones((t, t), bool), k=1)
            scores = jnp.where(mask, -jnp.inf, scores)
            w = jax.nn.softmax(scores, axis=-1)
            ctx = jnp.einsum('bhqk,bhkd->bhqd', w, v).transpose(0, 2, 1, 3).reshape(b, t, d)
            return ctx @ Wp + bp

        def _mlp(x, W1, b1, W2, b2):
            return jax.nn.silu(x @ W1 + b1) @ W2 + b2
        key = jax.random.key(seed)
        ks = jax.random.split(key, 12)
        s = lambda fan_in: 1.0 / np.sqrt(fan_in)
        return {'x': jax.random.normal(ks[0], (B, T, D), jnp.float32), 'c': jax.random.normal(ks[1], (B, D), jnp.float32), 'Wq': jax.random.normal(ks[2], (D, D), jnp.float32) * s(D), 'Wk': jax.random.normal(ks[3], (D, D), jnp.float32) * s(D), 'Wv': jax.random.normal(ks[4], (D, D), jnp.float32) * s(D), 'Wp': jax.random.normal(ks[5], (D, D), jnp.float32) * s(D), 'bp': jnp.zeros((D,), jnp.float32), 'W1': jax.random.normal(ks[6], (D, 4 * D), jnp.float32) * s(D), 'b1': jnp.zeros((4 * D,), jnp.float32), 'W2': jax.random.normal(ks[7], (4 * D, D), jnp.float32) * s(4 * D), 'b2': jnp.zeros((D,), jnp.float32), 'Wa': jax.random.normal(ks[8], (D, 6 * D), jnp.float32) * s(D), 'ba': jnp.zeros((6 * D,), jnp.float32)}
    _L0_cond_all = _L0_cond_setup()
    _L0_cond_in = {k: v for k, v in _L0_cond_all.items() if k in ('Wq', 'Wk', 'Wv', 'Wp', 'bp', 'W1', 'b1', 'W2', 'b2', 'Wa', 'ba')}
    del _L0_cond_all

    def _L1_cond_setup():
        import jax, jax.numpy as jnp
        import numpy as np
        N, T, D, H = (32, 128, 144, 16)
        DH = D // H
        MLP = int(D * 4.0)
        EPS = 1e-06

        def _layernorm(x):
            m = jnp.mean(x, axis=-1, keepdims=True)
            v = jnp.var(x, axis=-1, keepdims=True)
            return (x - m) * jax.lax.rsqrt(v + EPS)

        def _modulate(x, shift, scale):
            return x * (1.0 + scale[:, None, :]) + shift[:, None, :]

        def _attention(x, qkv_w, qkv_b, proj_w, proj_b):
            n, t, d = x.shape
            scale = DH ** (-0.5)
            qkv = x @ qkv_w + qkv_b
            qkv = qkv.reshape(n, t, 3, H, DH)
            q, k, v = (qkv[:, :, 0], qkv[:, :, 1], qkv[:, :, 2])
            attn = jnp.einsum('nthd,ntkd->nthk', q * scale, k)
            attn = jax.nn.softmax(attn, axis=-1)
            out = jnp.einsum('nthk,ntkd->nthd', attn, v)
            out = out.transpose(0, 2, 1, 3).reshape(n, t, d)
            return out @ proj_w + proj_b

        def _mlp(x, fc1_w, fc1_b, fc2_w, fc2_b):
            h = jax.nn.gelu(x @ fc1_w + fc1_b, approximate=False)
            return h @ fc2_w + fc2_b
        key = jax.random.key(seed)
        ks = jax.random.split(key, 14)
        s = 0.02
        return {'x': jax.random.normal(ks[0], (N, T, D), jnp.float32), 'c': jax.random.normal(ks[1], (N, D), jnp.float32), 'qkv_w': jax.random.normal(ks[2], (D, 3 * D), jnp.float32) * s, 'qkv_b': jax.random.normal(ks[3], (3 * D,), jnp.float32) * s, 'proj_w': jax.random.normal(ks[4], (D, D), jnp.float32) * s, 'proj_b': jax.random.normal(ks[5], (D,), jnp.float32) * s, 'fc1_w': jax.random.normal(ks[6], (D, MLP), jnp.float32) * s, 'fc1_b': jax.random.normal(ks[7], (MLP,), jnp.float32) * s, 'fc2_w': jax.random.normal(ks[8], (MLP, D), jnp.float32) * s, 'fc2_b': jax.random.normal(ks[9], (D,), jnp.float32) * s, 'ada_w': jax.random.normal(ks[10], (D, 6 * D), jnp.float32) * s, 'ada_b': jax.random.normal(ks[11], (6 * D,), jnp.float32) * s}
    _L1_cond_all = _L1_cond_setup()
    _L1_cond_in = {k: v for k, v in _L1_cond_all.items() if k in ('qkv_w', 'qkv_b', 'proj_w', 'proj_b', 'fc1_w', 'fc1_b', 'fc2_w', 'fc2_b', 'ada_w', 'ada_b')}
    del _L1_cond_all
    return {'x': x, 'cond_1152': cond_1152, 'L0_cond_Wq': _L0_cond_in['Wq'], 'L0_cond_Wk': _L0_cond_in['Wk'], 'L0_cond_Wv': _L0_cond_in['Wv'], 'L0_cond_Wp': _L0_cond_in['Wp'], 'L0_cond_bp': _L0_cond_in['bp'], 'L0_cond_W1': _L0_cond_in['W1'], 'L0_cond_b1': _L0_cond_in['b1'], 'L0_cond_W2': _L0_cond_in['W2'], 'L0_cond_b2': _L0_cond_in['b2'], 'L0_cond_Wa': _L0_cond_in['Wa'], 'L0_cond_ba': _L0_cond_in['ba'], 'L1_cond_qkv_w': _L1_cond_in['qkv_w'], 'L1_cond_qkv_b': _L1_cond_in['qkv_b'], 'L1_cond_proj_w': _L1_cond_in['proj_w'], 'L1_cond_proj_b': _L1_cond_in['proj_b'], 'L1_cond_fc1_w': _L1_cond_in['fc1_w'], 'L1_cond_fc1_b': _L1_cond_in['fc1_b'], 'L1_cond_fc2_w': _L1_cond_in['fc2_w'], 'L1_cond_fc2_b': _L1_cond_in['fc2_b'], 'L1_cond_ada_w': _L1_cond_in['ada_w'], 'L1_cond_ada_b': _L1_cond_in['ada_b']}

def reference(x, cond_1152, L0_cond_Wq, L0_cond_Wk, L0_cond_Wv, L0_cond_Wp, L0_cond_bp, L0_cond_W1, L0_cond_b1, L0_cond_W2, L0_cond_b2, L0_cond_Wa, L0_cond_ba, L1_cond_qkv_w, L1_cond_qkv_b, L1_cond_proj_w, L1_cond_proj_b, L1_cond_fc1_w, L1_cond_fc1_b, L1_cond_fc2_w, L1_cond_fc2_b, L1_cond_ada_w, L1_cond_ada_b):
    import jax
    import jax.numpy as jnp

    def _L0_cond_ref(x, c, Wq, Wk, Wv, Wp, bp, W1, b1, W2, b2, Wa, ba):
        import jax, jax.numpy as jnp
        import numpy as np
        B, T, D, H = (64, 32, 144, 16)
        HD = D // H
        EPS = 1e-06

        def _ln(x):
            mu = jnp.mean(x, axis=-1, keepdims=True)
            var = jnp.var(x, axis=-1, keepdims=True)
            return (x - mu) * jax.lax.rsqrt(var + EPS)

        def _modulate(x, shift, scale):
            return x * (1.0 + scale[:, None, :]) + shift[:, None, :]

        def _attn(x, Wq, Wk, Wv, Wp, bp):
            b, t, d = x.shape
            q = (x @ Wq).reshape(b, t, H, HD).transpose(0, 2, 1, 3)
            k = (x @ Wk).reshape(b, t, H, HD).transpose(0, 2, 1, 3)
            v = (x @ Wv).reshape(b, t, H, HD).transpose(0, 2, 1, 3)
            scores = jnp.einsum('bhqd,bhkd->bhqk', q, k) / np.sqrt(HD)
            mask = jnp.triu(jnp.ones((t, t), bool), k=1)
            scores = jnp.where(mask, -jnp.inf, scores)
            w = jax.nn.softmax(scores, axis=-1)
            ctx = jnp.einsum('bhqk,bhkd->bhqd', w, v).transpose(0, 2, 1, 3).reshape(b, t, d)
            return ctx @ Wp + bp

        def _mlp(x, W1, b1, W2, b2):
            return jax.nn.silu(x @ W1 + b1) @ W2 + b2
        mod = jax.nn.silu(c) @ Wa + ba
        sh_msa, sc_msa, g_msa, sh_mlp, sc_mlp, g_mlp = jnp.split(mod, 6, axis=1)
        x = x + g_msa[:, None, :] * _attn(_modulate(_ln(x), sh_msa, sc_msa), Wq, Wk, Wv, Wp, bp)
        x = x + g_mlp[:, None, :] * _mlp(_modulate(_ln(x), sh_mlp, sc_mlp), W1, b1, W2, b2)
        return x

    def _L1_cond_ref(x, c, qkv_w, qkv_b, proj_w, proj_b, fc1_w, fc1_b, fc2_w, fc2_b, ada_w, ada_b):
        import jax, jax.numpy as jnp
        import numpy as np
        N, T, D, H = (32, 128, 144, 16)
        DH = D // H
        MLP = int(D * 4.0)
        EPS = 1e-06

        def _layernorm(x):
            m = jnp.mean(x, axis=-1, keepdims=True)
            v = jnp.var(x, axis=-1, keepdims=True)
            return (x - m) * jax.lax.rsqrt(v + EPS)

        def _modulate(x, shift, scale):
            return x * (1.0 + scale[:, None, :]) + shift[:, None, :]

        def _attention(x, qkv_w, qkv_b, proj_w, proj_b):
            n, t, d = x.shape
            scale = DH ** (-0.5)
            qkv = x @ qkv_w + qkv_b
            qkv = qkv.reshape(n, t, 3, H, DH)
            q, k, v = (qkv[:, :, 0], qkv[:, :, 1], qkv[:, :, 2])
            attn = jnp.einsum('nthd,ntkd->nthk', q * scale, k)
            attn = jax.nn.softmax(attn, axis=-1)
            out = jnp.einsum('nthk,ntkd->nthd', attn, v)
            out = out.transpose(0, 2, 1, 3).reshape(n, t, d)
            return out @ proj_w + proj_b

        def _mlp(x, fc1_w, fc1_b, fc2_w, fc2_b):
            h = jax.nn.gelu(x @ fc1_w + fc1_b, approximate=False)
            return h @ fc2_w + fc2_b
        ada = jax.nn.silu(c) @ ada_w + ada_b
        shift_msa, scale_msa, gate_msa, shift_mlp, scale_mlp, gate_mlp = jnp.split(ada, 6, axis=1)
        x = x + gate_msa[:, None, :] * _attention(_modulate(_layernorm(x), shift_msa, scale_msa), qkv_w, qkv_b, proj_w, proj_b)
        x = x + gate_mlp[:, None, :] * _mlp(_modulate(_layernorm(x), shift_mlp, scale_mlp), fc1_w, fc1_b, fc2_w, fc2_b)
        return x
    x = _L0_cond_ref(x, cond_1152, L0_cond_Wq, L0_cond_Wk, L0_cond_Wv, L0_cond_Wp, L0_cond_bp, L0_cond_W1, L0_cond_b1, L0_cond_W2, L0_cond_b2, L0_cond_Wa, L0_cond_ba)
    x = _L1_cond_ref(x, cond_1152, L1_cond_qkv_w, L1_cond_qkv_b, L1_cond_proj_w, L1_cond_proj_b, L1_cond_fc1_w, L1_cond_fc1_b, L1_cond_fc2_w, L1_cond_fc2_b, L1_cond_ada_w, L1_cond_ada_b)
    return x

_drawn_inputs = setup_inputs


def setup_inputs(seed=0):
    import zlib

    import numpy as np

    out = dict(_drawn_inputs(seed))
    spreads = {'L0_cond_bp': (0.0, 0.1),
     'L0_cond_b1': (0.0, 0.1),
     'L0_cond_b2': (0.0, 0.1),
     'L0_cond_ba': (0.0, 0.1)}
    factors = {'L1_cond_qkv_w': 8.0,
     'L1_cond_qkv_b': 8.0,
     'L1_cond_proj_w': 8.0,
     'L1_cond_proj_b': 8.0,
     'L1_cond_fc1_w': 8.0,
     'L1_cond_fc1_b': 8.0,
     'L1_cond_fc2_w': 8.0,
     'L1_cond_fc2_b': 34.026,
     'L1_cond_ada_w': 7.189,
     'L1_cond_ada_b': 8.0}
    for name, (base, spread) in spreads.items():
        noise = np.random.default_rng([zlib.crc32(name.encode()), seed]).standard_normal(out[name].shape)
        drawn = base * np.exp(spread * noise) if base else spread * noise
        out[name] = jnp.asarray(drawn.astype(out[name].dtype))
    for name, factor in factors.items():
        out[name] = (out[name] * factor).astype(out[name].dtype)
    return out
```

```python
import concourse.bass as bass
from concourse import mybir
from contextlib import ExitStack

F32 = mybir.dt.float32
BF16 = mybir.dt.bfloat16
ALU = mybir.AluOpType
ACT = mybir.ActivationFunctionType
AX = mybir.AxisListType

NSEQ, SEQ, D = 32, 32, 144
H = 16
HD = D // H
P = 128
TILES = NSEQ * SEQ // P
SEQS = P // SEQ
KC = 2
KP = D // KC
HG = 4
GW = HG * HD
MLP = 4 * D
MC = (MLP + P - 1) // P
ML = MLP - (MC - 1) * P
NMOD = 6
EPS = 1e-6
SCALE = 1.0 / 3.0
MASKED = -1e30
LO, HI = 0, 64
SHIFT_A, SCALE_A, GATE_A, SHIFT_M, SCALE_M, GATE_M = range(NMOD)

C_ID = 0
C_KM = C_ID + P
C_SEL = C_KM + HG
C_CAUSAL = C_SEL + P
C_TILE = C_CAUSAL + 8 * SEQ
C_ALL = C_TILE + TILES * P


def constants():
    import numpy as np
    c = np.zeros((P, C_ALL), np.float32)
    c[:, C_ID:C_ID + P] = np.eye(P)
    for base in (LO, HI):
        for r in range(GW):
            c[base + r, C_KM + r // HD] = 1.0
    for r in range(SEQ):
        c[r, C_SEL + r:C_SEL + P:SEQ] = 1.0
        for blk in range(8):
            c[r, C_CAUSAL + blk * SEQ + r + 1:C_CAUSAL + (blk + 1) * SEQ] = MASKED
    for s in range(3):
        for t in range(TILES):
            for j in range(SEQS):
                c[32 * s + SEQS * t + j, C_TILE + t * P + j * SEQ:C_TILE + t * P + (j + 1) * SEQ] = 1.0
    return c


def build(nc, x, cond, w, consts, out):
    ctx = ExitStack()
    with ctx:
        def sb(name, shape, dt=F32):
            return ctx.enter_context(nc.sbuf_tensor(name, shape, dt))

        def pb(name):
            return ctx.enter_context(nc.psum_tensor(name, [P, 512], F32))

        def sem(name):
            return ctx.enter_context(nc.semaphore(name))

        X = sb("X", [P, TILES, D])
        MOD = sb("MOD", [P, TILES, 2 * NMOD, D])
        CST = sb("CST", [P, C_ALL])
        selb = sb("selb", [SEQ, P], BF16)
        causalb = sb("causalb", [SEQ, 8 * SEQ], BF16)
        tileb = sb("tileb", [96, TILES, P], BF16)
        ident = CST[:, C_ID:C_ID + P]
        kmask = CST[:, C_KM:C_KM + HG]
        cnd = sb("cnd", [NSEQ, D])
        cth = sb("cth", [NSEQ, D])
        csl = sb("csl", [NSEQ, D])
        cT = sb("cT", [KP + 1, KC, 96])
        wa = [sb(f"wa{i}", [KP + 1, KC, NMOD * D]) for i in range(2)]
        mods = [sb(f"mods{i}", [96, NMOD * D]) for i in range(2)]
        rest = [sb(f"rest{i}", [96, NMOD * D]) for i in range(2)]
        part = [[sb(f"part{i}_{j}", [96, NMOD * D], BF16) for j in range(3)] for i in range(2)]
        stack = [sb(f"stack{i}", [96, NMOD * D], BF16) for i in range(2)]

        wq = sb("wq", [KP, KC, D])
        wk = sb("wk", [KP, KC, D])
        wv = sb("wv", [KP, KC, D])
        wp0 = sb("wp0", [KP + 1, KC, D])
        wqkv = sb("wqkv", [KP + 1, KC, 3 * D])
        wp1 = sb("wp1", [P, 5, D])
        w1 = [sb(f"w1_{i}", [KP + 1, KC, MLP]) for i in range(2)]
        w2 = [sb(f"w2_{i}", [P, MC, D]) for i in range(2)]

        epst = sb("epst", [P, 1])
        mhalf = sb("mhalf", [P, 1])
        LN = range(4)
        st = [sb(f"st{i}", [P, 6]) for i in LN]
        mv = [sb(f"mv{i}", [P, 2]) for i in LN]
        ve = [sb(f"ve{i}", [P, 1]) for i in LN]
        rstd = [sb(f"rstd{i}", [P, 1]) for i in LN]
        u = [sb(f"u{i}", [P, D]) for i in LN]
        xm = [sb(f"xm{i}", [P, D]) for i in LN]
        xmT = [sb(f"xmT{i}", [KP + 1, KC, P]) for i in LN]
        g = [sb(f"g{i}", [P, D]) for i in range(4)]
        th = sb("th", [P, MC, P])
        hT = [sb(f"hT{i}", [P, MC, P]) for i in range(2)]

        qT = sb("qT", [HI + GW, 2, P])
        Kx = sb("Kx", [HI + GW, 2, SEQS, HG, SEQ])
        Vx = sb("Vx", [P, SEQS, HG, HG, HD + 1])
        mx0 = sb("mx0", [P, H])
        s0 = sb("s0", [P, H, SEQ])
        p0 = sb("p0", [P, H, SEQ])
        pT = sb("pT", [P, HG, P])
        rs0 = sb("rs0", [P, H])
        ctx0 = sb("ctx0", [P, D])
        ctxT = sb("ctxT", [KP + 1, KC, P])

        qkv = sb("qkv", [P, 3 * D])
        pq = sb("pq", [P, H, H, HD])
        s1 = sb("s1", [P, H, H])
        mx1 = sb("mx1", [P, H])
        e1 = sb("e1", [P, H, H])
        p1 = sb("p1", [P, H, H])
        rs1 = sb("rs1", [P, H])
        ri1 = sb("ri1", [P, H])
        pa = sb("pa", [P, H, HD, H])
        o1 = sb("o1", [P, H, HD])
        ctx1 = sb("ctx1", [P, HD, 32])
        y1 = sb("y1", [P, 2, 160])
        y2 = sb("y2", [P, 5, 64])

        a0, a1, a2, b0, b1, c0, d0, d1 = [pb(n) for n in ("a0", "a1", "a2", "b0", "b1", "c0", "d0", "d1")]

        load = {n: sem("load_" + n) for n in ("x", "c", "cst", "wa0", "wa1", "qkv0", "mlp0", "qkv1", "mlp1")}
        S = {}
        for n in ("act_c dve_c1 dve_c2 pe_cT act_cT pe_mod0 pe_mod1 act_mod0 act_mod1 dve_st dve_stack0 dve_stack1 "
                  "setup dve_cast pe_rep rep_act rep_dve w2half order_pe order_dve "
                  "stats0 stats1 stats2 stats3 var0 var1 var2 var3 pool_ve0 pool_ve1 pool_ve2 pool_ve3 "
                  "rstd0 rstd1 rstd2 rstd3 cen0 cen1 cen2 cen3 xm0 xm1 xm2 xm3 "
                  "pe_xT0 pe_xT1 pe_xT2 pe_xT3 act_xT0 act_xT1 act_xT2 act_xT3 "
                  "pe_v act_v pe_qk act_q act_k pe_s dve_mx dve_s act_p "
                  "pe_pT act_pT pe_av dve_rs dve_ctx pe_cxT act_cxT pe_pr0 dve_g0 dve_x1 "
                  "pe_up0 act_th dve_h pe_dn0 dve_g1 dve_x2 "
                  "pe_qkv act_qkv pool_pq dve_s1 dve_mx1 dve_e1 act_p1 dve_sum1 dve_ri1 "
                  "pool_pa dve_o1 dve_ctx1 dve_y1 dve_y2 pe_pr1 dve_g2 dve_x3 "
                  "pe_up1 act_h1 pe_dn1 dve_g3 dve_xo out").split():
            S[n] = sem(n)

        def tile(ap, t):
            return ap[:, bass.ds(t, 1)]

        def xt(t):
            return X[:, bass.ds(t, 1), :].rearrange("p a f -> p (a f)")

        def mod(t, k):
            return MOD[:, bass.ds(t, 1), k, :].rearrange("p a f -> p (a f)")

        block = ctx.enter_context(nc.Block())

        @block.sync
        def _(sp):
            sp.dma_start(cnd[:], cond).then_inc(load["c"], 16)
            sp.dma_start(CST[:], consts).then_inc(load["cst"], 16)
            for n, i, wname, bname in (("wa0", 0, "L0_cond_Wa", "L0_cond_ba"), ("wa1", 1, "L1_cond_ada_w", "L1_cond_ada_b")):
                sp.wait_ge(S["setup"], 1)
                sp.dma_start(wa[i][0:KP], w[wname].rearrange("(k p) n -> p k n", p=KP)).then_inc(load[n], 16)
                sp.dma_start(wa[i][KP:KP + 1, 0, :], w[bname].rearrange("(a n) -> a n", a=1)).then_inc(load[n], 16)
                if i == 0:
                    sp.dma_start(X[:], x.rearrange("b s f -> (b s) f").rearrange("(t p) f -> p t f", p=P)).then_inc(load["x"], 16)
                    for dst, name in ((wq, "L0_cond_Wq"), (wk, "L0_cond_Wk"), (wv, "L0_cond_Wv"), (wp0, "L0_cond_Wp")):
                        sp.dma_start(dst[0:KP], w[name].rearrange("(k p) n -> p k n", p=KP)).then_inc(load["qkv0"], 16)
                    sp.dma_start(wp0[KP:KP + 1, 0, :], w["L0_cond_bp"].rearrange("(a n) -> a n", a=1)).then_inc(load["qkv0"], 16)

            with sp.Fori(0, TILES) as t:
                sp.wait_ge(S["dve_xo"], t + 1)
                sp.dma_start(out.rearrange("b s f -> (b s) f").rearrange("(t p) f -> p t f", p=P)[:, bass.ds(t, 1), :],
                             X[:, bass.ds(t, 1), :]).then_inc(S["out"], 16)
            sp.wait_ge(S["out"], 16 * TILES)

        @block.gpsimd
        def _(pool):
            pool.wait_ge(S["setup"], 1)
            mlp = (("mlp0", 0, "L0_cond_W1", "L0_cond_b1", "L0_cond_W2", "L0_cond_b2"),
                   ("mlp1", 1, "L1_cond_fc1_w", "L1_cond_fc1_b", "L1_cond_fc2_w", "L1_cond_fc2_b"))
            for n, i, a, ab, b, bb in mlp:
                pool.dma_start(w1[i][0:KP], w[a].rearrange("(k p) n -> p k n", p=KP)).then_inc(load[n], 16)
                pool.dma_start(w1[i][KP:KP + 1, 0, :], w[ab].rearrange("(a n) -> a n", a=1)).then_inc(load[n], 16)
                pool.dma_start(w2[i][:, 0:MC - 1, :], w[b][0:(MC - 1) * P].rearrange("(k p) n -> p k n", p=P)).then_inc(load[n], 16)
                pool.dma_start(w2[i][0:ML, MC - 1, :], w[b][(MC - 1) * P:MLP]).then_inc(load[n], 16)
                pool.dma_start(w2[i][ML:ML + 1, MC - 1, :], w[bb].rearrange("(a n) -> a n", a=1)).then_inc(load[n], 16)
                if i == 0:
                    pool.dma_start(wqkv[0:KP], w["L1_cond_qkv_w"].rearrange("(k p) n -> p k n", p=KP)).then_inc(load["qkv1"], 16)
                    pool.dma_start(wqkv[KP:KP + 1, 0, :], w["L1_cond_qkv_b"].rearrange("(a n) -> a n", a=1)).then_inc(load["qkv1"], 16)
                    wp = w["L1_cond_proj_w"].rearrange("(l d) n -> l d n", d=HD)
                    for s in range(SEQS):
                        for odd in range(2):
                            at = 32 * s + 16 * odd
                            pool.dma_start(wp1[at:at + 16, 0:5 - odd, :], wp[:, odd:HD:2, :]).then_inc(load["qkv1"], 16)
                        pool.dma_start(wp1[32 * s + 16:32 * s + 17, 4, :],
                                       w["L1_cond_proj_b"].rearrange("(a n) -> a n", a=1)).then_inc(load["qkv1"], 16)

            def rsqrt(n, i):
                pool.wait_ge(S[f"var{i}"], n)
                nc.gpsimd.tensor_tensor(ve[i][:], mv[i][:, 1:2], epst[:], ALU.add).then_inc(S[f"pool_ve{i}"], 1)
                pool.wait_ge(S[f"pool_ve{i}"], n)
                nc.gpsimd.tensor_tensor(rstd[i][:], ve[i][:], mhalf[:], ALU.pow).then_inc(S[f"rstd{i}"], 1)

            with pool.Fori(0, TILES) as t:
                n = t + 1
                rsqrt(n, 0)
                rsqrt(n, 1)
                rsqrt(n, 2)
                pool.wait_ge(S["act_qkv"], n)
                q = qkv[:, 0:D].rearrange("p (h d) -> p h d", d=HD)
                k = qkv[:, D:2 * D].rearrange("p (h d) -> p h d", d=HD)
                v = qkv[:, 2 * D:3 * D].rearrange("p (h d) -> p d h", d=HD)
                nc.gpsimd.tensor_tensor(pq[:], q.unsqueeze(2).broadcast_to([P, H, H, HD]),
                                        k.unsqueeze(1).broadcast_to([P, H, H, HD]), ALU.mult).then_inc(S["pool_pq"], 1)
                pool.wait_ge(S["act_p1"], n)
                nc.gpsimd.tensor_tensor(pa[:], p1[:].unsqueeze(2).broadcast_to([P, H, HD, H]),
                                        v.unsqueeze(1).broadcast_to([P, H, HD, H]), ALU.mult).then_inc(S["pool_pa"], 1)
                rsqrt(n, 3)

        @block.scalar
        def _(act):
            act.wait_ge(load["c"], 16)
            nc.scalar.activation(cth[:], cnd[:], ACT.Tanh, scale=0.5).then_inc(S["act_c"], 1)
            act.wait_ge(S["pe_cT"], 1)
            act.wait_ge(S["setup"], 1)
            nc.scalar.activation(cT[0:KP], a0[0:KP, 0:KC * NSEQ].rearrange("p (k b) -> p k b", k=KC).unsqueeze(2)
                                 .broadcast_to([KP, KC, 3, NSEQ]), ACT.Copy).then_inc(S["act_cT"], 1)
            for i in range(2):
                act.wait_ge(S[f"pe_mod{i}"], 1)
                for k in range(NMOD):
                    ps = ((a0, a1), (b0, b1))[i][k // 3]
                    nc.scalar.activation(mods[i][:, k * D:(k + 1) * D], ps[0:96, (k % 3) * D:(k % 3 + 1) * D],
                                         ACT.Copy, bias=1.0 if k in (SCALE_A, SCALE_M) else 0.0
                                         ).then_inc(S[f"act_mod{i}"], 1)
            for r in range(0, 2 * 2 * TILES, 2):
                act.wait_ge(S["pe_rep"], r + 1)
                i, t, half = r // (2 * TILES), r // 2 % TILES, r % 2
                nc.scalar.activation(MOD[:, t, NMOD * i + 3 * half:NMOD * i + 3 * half + 3, :]
                                     .rearrange("p k f -> p (k f)"), a0[:, 0:3 * D], ACT.Copy).then_inc(S["rep_act"], 1)

            def evac_xT(n, i, ps):
                act.wait_ge(S[f"pe_xT{i}"], n)
                nc.scalar.activation(xmT[i][0:KP].rearrange("p k t -> p (k t)"), ps[0:KP, 0:KC * P], ACT.Copy
                                     ).then_inc(S[f"act_xT{i}"], 1)

            with act.Fori(0, TILES) as t:
                n = t + 1
                evac_xT(n, 0, a0)
                act.wait_ge(S["pe_v"], n)
                for h in range(HG):
                    r = slice(32 * h, 32 * h + 32)
                    last = nc.scalar.activation(Vx[r, :, :, h, 0:HD].rearrange("p b g d -> p (b g) d"),
                                                a1[r, 0:D].rearrange("p (a d) -> p a d", d=HD), ACT.Copy)
                last.then_inc(S["act_v"], 1)
                act.wait_ge(S["pe_qk"], n)
                nc.scalar.activation(qT[:].rearrange("p j t -> p (j t)"), a0[0:HI + GW, 0:2 * P], ACT.Copy
                                     ).then_inc(S["act_q"], 1)
                for h in range(HG):
                    last = nc.scalar.activation(
                        Kx[:, :, :, h, :].rearrange("p j b k -> p (j b) k"),
                        a0[0:HI + GW, 2 * P:4 * P].rearrange("p (a k) -> p a k", k=SEQ), ACT.Copy,
                        scale=kmask[0:HI + GW, h:h + 1])
                last.then_inc(S["act_k"], 1)
                act.wait_ge(S["dve_s"], n)
                nc.scalar.activation(p0[:], s0[:], ACT.Exp, scale=SCALE).then_inc(S["act_p"], 1)
                act.wait_ge(S["pe_pT"], n)
                nc.scalar.activation(pT[:].rearrange("p g t -> p (g t)"), b0[:], ACT.Copy).then_inc(S["act_pT"], 1)
                act.wait_ge(S["pe_cxT"], n)
                nc.scalar.activation(ctxT[0:KP].rearrange("p k t -> p (k t)"), b0[0:KP, 0:KC * P], ACT.Copy
                                     ).then_inc(S["act_cxT"], 1)
                evac_xT(n, 1, b0)
                act.wait_ge(S["pe_up0"], n)
                nc.scalar.activation(th[:, 0:MC - 1, :].rearrange("p m t -> p (m t)"), b0[:], ACT.Tanh, scale=0.5)
                nc.scalar.activation(th[0:ML, MC - 1, :], b1[0:ML, 0:P], ACT.Tanh, scale=0.5).then_inc(S["act_th"], 1)
                evac_xT(n, 2, c0)
                act.wait_ge(S["pe_qkv"], n)
                nc.scalar.activation(qkv[:], c0[:, 0:3 * D], ACT.Copy).then_inc(S["act_qkv"], 1)
                act.wait_ge(S["dve_e1"], n)
                nc.scalar.activation(p1[:], e1[:], ACT.Exp, scale=SCALE).then_inc(S["act_p1"], 1)
                evac_xT(n, 3, d0)
                act.wait_ge(S["pe_up1"], n)
                nc.scalar.activation(hT[1][:, 0:MC - 1, :].rearrange("p m t -> p (m t)"), d0[:], ACT.Gelu)
                nc.scalar.activation(hT[1][0:ML, MC - 1, :], d1[0:ML, 0:P], ACT.Gelu).then_inc(S["act_h1"], 1)

        @block.vector
        def _(dve):
            for ap, val in ((cT, 1.0), (ctxT, 1.0), (Vx, 0.0), (epst, EPS), (mhalf, -0.5), (ctx1, 0.0), (y1, 0.0),
                            *((xmT[i], 1.0) for i in LN)):
                nc.vector.memset(ap[:], val)
            nc.vector.memset(hT[0][ML:ML + 1, MC - 1, :], 1.0)
            nc.vector.memset(hT[1][ML:ML + 1, MC - 1, :], 1.0).then_inc(S["order_dve"], 1)
            dve.wait_ge(S["order_dve"], 1)
            for h in range(HG):
                nc.vector.memset(Vx[32 * h:32 * h + 32, :, :, h, HD:HD + 1], 1.0)
            nc.vector.memset(y1[:, :, D:D + 1], 1.0).then_inc(S["setup"], 1)
            dve.wait_ge(load["cst"], 16)
            nc.vector.tensor_copy(selb[:], CST[0:SEQ, C_SEL:C_SEL + P])
            nc.vector.tensor_copy(causalb[:], CST[0:SEQ, C_CAUSAL:C_CAUSAL + 8 * SEQ])
            nc.vector.tensor_copy(tileb[:].rearrange("p t q -> p (t q)"), CST[0:96, C_TILE:C_TILE + TILES * P]
                                  ).then_inc(S["dve_cast"], 1)
            dve.wait_ge(S["act_c"], 1)
            nc.vector.scalar_tensor_tensor(cth[:], cth[:], 1.0, cnd[:], ALU.add, ALU.mult).then_inc(S["dve_c1"], 1)
            dve.wait_ge(S["dve_c1"], 1)
            nc.vector.tensor_scalar_mul(csl[:], cth[:], 0.5).then_inc(S["dve_c2"], 1)
            k = 0
            for i in range(2):
                dve.wait_ge(S[f"act_mod{i}"], NMOD)
                src = mods[i]
                for j in range(3):
                    nc.vector.tensor_copy(part[i][j][:], src[:]).then_inc(S["dve_st"], 1)
                    k += 1
                    dve.wait_ge(S["dve_st"], k)
                    r = slice(32 * j, 32 * j + 32)
                    last = nc.vector.tensor_copy(stack[i][r, :], part[i][j][r, :])
                    if j < 2:
                        nc.vector.tensor_tensor(rest[i][:], src[:], part[i][j][:], ALU.subtract).then_inc(S["dve_st"], 1)
                        k += 1
                        dve.wait_ge(S["dve_st"], k)
                        src = rest[i]
                last.then_inc(S[f"dve_stack{i}"], 1)
            for r in range(1, 2 * 2 * TILES, 2):
                dve.wait_ge(S["pe_rep"], r + 1)
                i, t, half = r // (2 * TILES), r // 2 % TILES, r % 2
                nc.vector.tensor_copy(MOD[:, t, NMOD * i + 3 * half:NMOD * i + 3 * half + 3, :]
                                      .rearrange("p k f -> p (k f)"), b0[:, 0:3 * D]).then_inc(S["rep_dve"], 1)
            dve.wait_ge(S["rep_act"], 2 * TILES)
            dve.wait_ge(S["rep_dve"], 2 * TILES)
            dve.wait_ge(load["mlp0"], 5 * 16)
            nc.vector.tensor_scalar_mul(w2[0][:, 0:MC - 1, :], w2[0][:, 0:MC - 1, :], 0.5)
            nc.vector.tensor_scalar_mul(w2[0][0:ML, MC - 1, :], w2[0][0:ML, MC - 1, :], 0.5).then_inc(S["w2half"], 1)
            dve.wait_ge(load["x"], 16)

            def norm(t, n, i, src, shift, scale):
                nc.vector.bn_stats(st[i][:], src).then_inc(S[f"stats{i}"], 1)
                dve.wait_ge(S[f"stats{i}"], n)
                dve.sem_inc(S["order_dve"], 1)
                nc.vector.bn_aggr(mv[i][:], st[i][:]).then_inc(S[f"var{i}"], 1)
                dve.wait_ge(S[f"var{i}"], n)
                nc.vector.scalar_tensor_tensor(u[i][:], src, mv[i][:, 0:1], mod(t, scale), ALU.subtract, ALU.mult
                                               ).then_inc(S[f"cen{i}"], 1)
                dve.wait_ge(S[f"rstd{i}"], n)
                dve.wait_ge(S[f"cen{i}"], n)
                nc.vector.scalar_tensor_tensor(xm[i][:], u[i][:], rstd[i][:], mod(t, shift), ALU.mult, ALU.add
                                               ).then_inc(S[f"xm{i}"], 1)

            def gated(t, n, i, done, ps, gate, src, dst, ready):
                dve.wait_ge(S[done], n)
                nc.vector.tensor_tensor(g[i][:], ps, mod(t, gate), ALU.mult).then_inc(S[f"dve_g{i}"], 1)
                dve.wait_ge(S[f"dve_g{i}"], n)
                nc.vector.tensor_tensor(dst, src, g[i][:], ALU.add).then_inc(S[ready], 1)
                dve.wait_ge(S[ready], n)
                dve.sem_inc(S["order_dve"], 1)

            with dve.Fori(0, TILES) as t:
                n = t + 1
                norm(t, n, 0, xt(t), SHIFT_A, SCALE_A)
                dve.wait_ge(S["pe_s"], n)
                banks = [ps[:, 0:8 * SEQ].rearrange("p (h k) -> p h k", k=SEQ) for ps in (a1, a2)]
                nc.vector.tensor_reduce(mx0[:, 0:8], banks[0], axis=AX.X, op=ALU.max)
                nc.vector.tensor_reduce(mx0[:, 8:16], banks[1], axis=AX.X, op=ALU.max).then_inc(S["dve_mx"], 1)
                dve.wait_ge(S["dve_mx"], n)
                for r in range(2):
                    last = nc.vector.tensor_tensor(s0[:, 8 * r:8 * r + 8, :], banks[r],
                                                   mx0[:, 8 * r:8 * r + 8].unsqueeze(2).broadcast_to([P, 8, SEQ]), ALU.subtract)
                last.then_inc(S["dve_s"], 1)
                dve.wait_ge(S["pe_av"], n)
                av = b1[:, 0:H * (HD + 1)].rearrange("p (h e) -> p h e", e=HD + 1)
                nc.vector.reciprocal(rs0[:].unsqueeze(2), av[:, :, HD:HD + 1]).then_inc(S["dve_rs"], 1)
                dve.wait_ge(S["dve_rs"], n)
                nc.vector.tensor_tensor(ctx0[:].rearrange("p (h d) -> p h d", d=HD), av[:, :, 0:HD],
                                        rs0[:].unsqueeze(2).broadcast_to([P, H, HD]), ALU.mult).then_inc(S["dve_ctx"], 1)
                gated(t, n, 0, "pe_pr0", b1[:, 0:D], GATE_A, xt(t), xt(t), "dve_x1")
                norm(t, n, 1, xt(t), SHIFT_M, SCALE_M)
                dve.wait_ge(S["act_th"], n)
                nc.vector.scalar_tensor_tensor(hT[0][:, 0:MC - 1, :].rearrange("p m t -> p (m t)"),
                                               th[:, 0:MC - 1, :].rearrange("p m t -> p (m t)"), 1.0, b0[:], ALU.add, ALU.mult)
                nc.vector.scalar_tensor_tensor(hT[0][0:ML, MC - 1, :], th[0:ML, MC - 1, :], 1.0, b1[0:ML, 0:P],
                                               ALU.add, ALU.mult).then_inc(S["dve_h"], 1)
                gated(t, n, 1, "pe_dn0", b1[:, 2 * P:2 * P + D], GATE_M, xt(t), xt(t), "dve_x2")

                norm(t, n, 2, xt(t), NMOD + SHIFT_A, NMOD + SCALE_A)
                dve.wait_ge(S["pool_pq"], n)
                nc.vector.tensor_reduce(s1[:], pq[:], axis=AX.X, op=ALU.add).then_inc(S["dve_s1"], 1)
                dve.wait_ge(S["dve_s1"], n)
                nc.vector.tensor_reduce(mx1[:], s1[:], axis=AX.X, op=ALU.max).then_inc(S["dve_mx1"], 1)
                dve.wait_ge(S["dve_mx1"], n)
                nc.vector.tensor_tensor(e1[:], s1[:], mx1[:].unsqueeze(2).broadcast_to([P, H, H]), ALU.subtract
                                        ).then_inc(S["dve_e1"], 1)
                dve.wait_ge(S["act_p1"], n)
                nc.vector.tensor_reduce(rs1[:], p1[:], axis=AX.X, op=ALU.add).then_inc(S["dve_sum1"], 1)
                dve.wait_ge(S["dve_sum1"], n)
                nc.vector.reciprocal(ri1[:], rs1[:]).then_inc(S["dve_ri1"], 1)
                dve.wait_ge(S["pool_pa"], n)
                nc.vector.tensor_reduce(o1[:], pa[:], axis=AX.X, op=ALU.add).then_inc(S["dve_o1"], 1)
                dve.wait_ge(S["dve_ri1"], n)
                dve.wait_ge(S["dve_o1"], n)
                nc.vector.tensor_tensor(ctx1[:, :, 0:H].rearrange("p d h -> p h d"), o1[:],
                                        ri1[:].unsqueeze(2).broadcast_to([P, H, HD]), ALU.mult).then_inc(S["dve_ctx1"], 1)
                dve.wait_ge(S["dve_ctx1"], n)
                nc.vector.transpose(y1[:, :, 0:D].rearrange("p a (d l) -> p d a l", l=16), ctx1[:]).then_inc(S["dve_y1"], 1)
                dve.wait_ge(S["dve_y1"], n)
                nc.vector.transpose(y2[:].rearrange("p j (c a) -> p a j c", a=2),
                                    y1[:].rearrange("p a (j x) -> p a j x", x=32)).then_inc(S["dve_y2"], 1)
                gated(t, n, 2, "pe_pr1", d1[:, 0:D], NMOD + GATE_A, xt(t), xt(t), "dve_x3")
                norm(t, n, 3, xt(t), NMOD + SHIFT_M, NMOD + SCALE_M)
                dve.wait_ge(S["pe_dn1"], n)
                nc.vector.tensor_tensor(g[3][:], d1[:, 2 * P:2 * P + D], mod(t, NMOD + GATE_M), ALU.mult
                                        ).then_inc(S["dve_g3"], 1)
                dve.wait_ge(S["dve_g3"], n)
                nc.vector.tensor_tensor(xt(t), xt(t), g[3][:], ALU.add).then_inc(S["dve_xo"], 1)

        @block.tensor
        def _(pe):
            mm = nc.tensor.matmul
            pe.wait_ge(load["cst"], 16)
            pe.wait_ge(S["dve_c2"], 1)
            for k in range(KC):
                last = nc.tensor.transpose(a0[0:KP, k * NSEQ:(k + 1) * NSEQ], csl[:, k * KP:(k + 1) * KP], ident[0:NSEQ, 0:NSEQ])
            last.then_inc(S["pe_cT"], 1)
            pe.wait_ge(S["act_cT"], 1)
            for i in range(2):
                pe.wait_ge(load[f"wa{i}"], 32)
                for half, ps in enumerate(((a0, a1), (b0, b1))[i]):
                    for k in range(KC):
                        r = KP + 1 - k
                        last = mm(ps[0:96, 0:3 * D], cT[0:r, k, :], wa[i][0:r, k, half * 3 * D:(half + 1) * 3 * D],
                                  start=k == 0, stop=k == KC - 1)
                last.then_inc(S[f"pe_mod{i}"], 1)
            pe.wait_ge(S["dve_cast"], 1)
            for r in range(2 * 2 * TILES):
                i, t, half = r // (2 * TILES), r // 2 % TILES, r % 2
                if r % (2 * TILES) == 0:
                    pe.wait_ge(S[f"dve_stack{i}"], 1)
                    pe.wait_ge(S["act_mod1"], NMOD)
                if r >= 2:
                    pe.wait_ge(S["rep_dve" if half else "rep_act"], r // 2)
                mm((b0 if half else a0)[:, 0:3 * D], tileb[:, t, :], stack[i][:, half * 3 * D:(half + 1) * 3 * D],
                   start=True, stop=True).then_inc(S["pe_rep"], 1)
            pe.wait_ge(S["rep_dve"], 2 * TILES)
            pe.wait_ge(S["rep_act"], 2 * TILES)

            def transpose(n, i, ps):
                pe.wait_ge(S[f"xm{i}"], n)
                for k in range(KC):
                    last = nc.tensor.transpose(ps[0:KP, k * P:(k + 1) * P], xm[i][:, k * KP:(k + 1) * KP], ident)
                last.then_inc(S[f"pe_xT{i}"], 1)

            def up(n, i, xi, big, small, done):
                pe.wait_ge(S[f"act_xT{xi}"], n)
                for m in range(MC):
                    w_ = P if m < MC - 1 else ML
                    dst = big[:, m * P:(m + 1) * P] if m < MC - 1 else small[0:ML, 0:P]
                    for k in range(KC):
                        r = KP + 1 - k
                        last = mm(dst, w1[i][0:r, k, m * P:m * P + w_], xmT[xi][0:r, k, :], start=k == 0, stop=k == KC - 1)
                last.then_inc(S[done], 1)

            def down(n, i, h, small, done):
                pe.wait_ge(S[h], n)
                for m in range(MC):
                    r = P if m < MC - 1 else ML + 1
                    last = mm(small[:, 2 * P:2 * P + D], hT[i][0:r, m, :], w2[i][0:r, m, :], start=m == 0, stop=m == MC - 1)
                last.then_inc(S[done], 1)

            pe.wait_ge(load["qkv0"], 5 * 16)
            pe.wait_ge(load["mlp0"], 5 * 16)
            pe.wait_ge(load["qkv1"], 14 * 16)
            pe.wait_ge(load["mlp1"], 5 * 16)
            pe.wait_ge(S["w2half"], 1)
            with pe.Fori(0, TILES) as t:
                n = t + 1
                transpose(n, 0, a0)
                pe.wait_ge(S["act_xT0"], n)
                for b in range(SEQS):
                    for k in range(KC):
                        for h in range(HG):
                            last = mm(a1[32 * h:32 * h + 32, b * GW:(b + 1) * GW], xmT[0][0:KP, k, b * SEQ:(b + 1) * SEQ],
                                      wv[:, k, :].rearrange("p (g h d) -> p g h d", g=HG, h=HG)[:, :, h, :],
                                      start=k == 0, stop=k == KC - 1)
                last.then_inc(S["pe_v"], 1)
                for which, wt in enumerate((wq, wk)):
                    for j in range(2):
                        for k in range(KC):
                            for r in range(2):
                                at = (2 * j + r) * GW
                                m = 64 if r == 0 else GW
                                col = (2 * which + j) * P
                                last = mm(a0[64 * r:64 * r + m, col:col + P], wt[:, k, at:at + m], xmT[0][0:KP, k, :],
                                          start=k == 0, stop=k == KC - 1)
                last.then_inc(S["pe_qk"], 1)
                pe.wait_ge(S["act_v"], n)
                pe.wait_ge(S["act_q"], n)
                pe.wait_ge(S["act_k"], n)
                for ps in (a1, a2):
                    mm(ps[:, 0:8 * SEQ], selb[:], causalb[:], start=True, stop=False, skip_group_check=True)
                for j in range(2):
                    for b in range(SEQS):
                        for r in range(2):
                            last = mm((a1, a2)[r][32 * b:32 * b + 32, j * P:(j + 1) * P],
                                      qT[64 * r:64 * r + GW, j, b * SEQ:(b + 1) * SEQ],
                                      Kx[64 * r:64 * r + GW, j, b].rearrange("p h k -> p (h k)"),
                                      start=False, stop=True, skip_group_check=True)
                last.then_inc(S["pe_s"], 1)
                pe.wait_ge(S["act_p"], n)
                for k in range(HG):
                    last = nc.tensor.transpose(b0[:, k * P:(k + 1) * P],
                                               p0[:, HG * k:HG * k + HG, :].rearrange("p h k -> p (h k)"), ident)
                last.then_inc(S["pe_pT"], 1)
                pe.wait_ge(S["act_pT"], n)
                for k in range(HG):
                    r, j = k // 2, k % 2
                    grp = 2 * j + r
                    for b in range(SEQS):
                        last = mm(b1[32 * b:32 * b + 32, grp * HG * (HD + 1):(grp + 1) * HG * (HD + 1)],
                                  pT[:, k, b * SEQ:(b + 1) * SEQ], Vx[:, b, grp].rearrange("p h e -> p (h e)"),
                                  start=True, stop=True)
                last.then_inc(S["pe_av"], 1)
                pe.wait_ge(S["dve_ctx"], n)
                for k in range(KC):
                    last = nc.tensor.transpose(b0[0:KP, k * P:(k + 1) * P], ctx0[:, k * KP:(k + 1) * KP], ident)
                last.then_inc(S["pe_cxT"], 1)
                pe.wait_ge(S["act_cxT"], n)
                for k in range(KC):
                    r = KP + 1 - k
                    last = mm(b1[:, 0:D], ctxT[0:r, k, :], wp0[0:r, k, :], start=k == 0, stop=k == KC - 1)
                last.then_inc(S["pe_pr0"], 1)
                transpose(n, 1, b0)
                up(n, 0, 1, b0, b1, "pe_up0")
                down(n, 0, "dve_h", b1, "pe_dn0")

                transpose(n, 2, c0)
                pe.wait_ge(S["act_xT2"], n)
                for k in range(KC):
                    r = KP + 1 - k
                    last = mm(c0[:, 0:3 * D], xmT[2][0:r, k, :], wqkv[0:r, k, :], start=k == 0, stop=k == KC - 1)
                last.then_inc(S["pe_qkv"], 1)
                pe.wait_ge(S["dve_y2"], n)
                pe.sem_inc(S["order_pe"], 1)
                for j in range(5):
                    rows = 32 if j < 4 else 17
                    for s in range(SEQS):
                        last = mm(d1[32 * s:32 * s + 32, 0:D],
                                  y2[32 * s:32 * s + rows, j, 0:SEQ],
                                  wp1[32 * s:32 * s + rows, j, :], start=j == 0, stop=j == 4)
                last.then_inc(S["pe_pr1"], 1)
                transpose(n, 3, d0)
                up(n, 1, 3, d0, d1, "pe_up1")
                down(n, 1, "act_h1", d1, "pe_dn1")


_W = ['L0_cond_Wq', 'L0_cond_Wk', 'L0_cond_Wv', 'L0_cond_Wp', 'L0_cond_bp', 'L0_cond_W1', 'L0_cond_b1', 'L0_cond_W2',
      'L0_cond_b2', 'L0_cond_Wa', 'L0_cond_ba', 'L1_cond_qkv_w', 'L1_cond_qkv_b', 'L1_cond_proj_w', 'L1_cond_proj_b',
      'L1_cond_fc1_w', 'L1_cond_fc1_b', 'L1_cond_fc2_w', 'L1_cond_fc2_b', 'L1_cond_ada_w', 'L1_cond_ada_b']


def kernel(**inputs):
    import numpy as _np
    import concourse.bacc as _bacc
    from concourse import mybir as _mybir
    from concourse.bass_utils import run_bass_kernel_spmd as _run

    nc = _bacc.Bacc("TRN2", target_bir_lowering=False, num_devices=1)
    arrays, aps = {}, {}
    for name in ['x', 'cond_1152', *_W]:
        a = _np.ascontiguousarray(inputs[name])
        arrays[f"in_{name}"] = a
        aps[name] = nc.dram_tensor(f"in_{name}", a.shape, _mybir.dt.from_np(a.dtype), kind="ExternalInput").ap()
    arrays["in_constants"] = constants()
    cst = nc.dram_tensor("in_constants", (P, C_ALL), F32, kind="ExternalInput").ap()
    out = nc.dram_tensor("out", (NSEQ, SEQ, D), F32, kind="ExternalOutput").ap()
    build(nc, aps["x"], aps["cond_1152"], {n: aps[n] for n in _W}, cst, out)
    r = _run(nc, [arrays], core_ids=[0])
    return r.results[0]["out"]
```

```python
import concourse.bass as bass
from concourse import mybir
from contextlib import ExitStack

F32 = mybir.dt.float32
BF16 = mybir.dt.bfloat16
ALU = mybir.AluOpType
ACT = mybir.ActivationFunctionType
AX = mybir.AxisListType

NSEQ, SEQ, D = 32, 32, 144
H = 16
HD = D // H
P = 128
TILES = NSEQ * SEQ // P
SEQS = P // SEQ
KC = 2
KP = D // KC
HG = 4
GW = HG * HD
REST = D + 1 - P
MLP = 4 * D
MC = (MLP + P - 1) // P
ML = MLP - (MC - 1) * P
NMOD = 6
EPS = 1e-6
SCALE = 1.0 / 3.0
MASKED = -1e30
LO, HI = 0, 64
SCALE_A = 1
MAX_LAG = 6
LOOP_FROM = 7



def head_rows():
    import numpy as np
    m = np.zeros((HI + GW, HG), np.float32)
    for r in range(GW):
        m[LO + r, r // HD] = m[HI + r, r // HD] = 1.0
    return m


def build(nc, x, cond, w, heads, out):
    ctx = ExitStack()
    with ctx:
        def sb(name, shape, dt=F32):
            return ctx.enter_context(nc.sbuf_tensor(name, shape, dt))

        def pb(name):
            return ctx.enter_context(nc.psum_tensor(name, [P, 512], F32))

        def sem(name):
            return ctx.enter_context(nc.semaphore(name))

        X = sb("X", [P, TILES, D])
        MOD = sb("MOD", [P, TILES, 2 * NMOD, D])
        QKV = sb("QKV", [P, TILES, 3 * D])
        P1 = sb("P1", [P, TILES, H * H])
        ident = sb("ident", [P, P])
        kmask = sb("kmask", [HI + GW, HG])
        selb = sb("selb", [SEQ, SEQS, SEQ], BF16)
        causalb = sb("causalb", [SEQ, 8, SEQ], BF16)
        tileb = sb("tileb", [96, TILES, SEQS, SEQ], BF16)
        cnd = sb("cnd", [NSEQ, D])
        cth = sb("cth", [NSEQ, D])
        cgt = sb("cgt", [NSEQ, D])
        csl = sb("csl", [NSEQ, D])
        cT = sb("cT", [KP + 1, KC, 96])
        wa = [sb(f"wa{i}", [KP + 1, KC, NMOD * D]) for i in range(2)]
        mods = [sb(f"mods{i}", [96, NMOD * D]) for i in range(2)]
        rest = sb("rest", [96, NMOD * D])
        midb = sb("midb", [96, NMOD * D], BF16)
        stack = [sb(f"stack{i}", [96, NMOD * D], BF16) for i in range(2)]

        wqk0 = sb("wqk0", [P, KC, 2, D])
        wqk = sb("wqk", [P, KC, 2, 2, HI + GW])
        wv = sb("wv", [P, KC, D])
        wp0 = sb("wp0", [P, KC, D])
        wqkv = sb("wqkv", [P, KC, 3 * D])
        wp1 = sb("wp1", [P, 5, D])
        w1 = [sb(f"w1_{i}", [P, KC, MLP]) for i in range(2)]
        w2 = [sb(f"w2_{i}", [P, MC, D]) for i in range(2)]

        epst = sb("epst", [P, 1])
        mhalf = sb("mhalf", [P, 1])
        LN = range(4)
        st = [sb(f"st{i}", [P, 6]) for i in LN]
        mv = [sb(f"mv{i}", [P, 2]) for i in LN]
        ve = [sb(f"ve{i}", [P, 1]) for i in LN]
        rstd = [sb(f"rstd{i}", [P, 1]) for i in LN]
        u = [sb(f"u{i}", [P, D]) for i in LN]
        xm = [sb(f"xm{i}", [P, KC * P]) for i in LN]
        xmT = [sb(f"xmT{i}", [P, KC, P]) for i in LN]
        g = [sb(f"g{i}", [P, D]) for i in range(4)]
        th = sb("th", [P, MC, P])
        hT = [sb(f"hT{i}", [P, MC, P]) for i in range(2)]

        qT = sb("qT", [HI + GW, 2, P])
        Kx = sb("Kx", [HI + GW, 2, SEQS, HG, SEQ])
        Vx = sb("Vx", [P, SEQS, HG, HG, HD + 1])
        mx0 = sb("mx0", [P, 2, 8])
        s0 = sb("s0", [P, 2, 8, SEQ])
        p0 = sb("p0", [P, 2, 8, SEQ])
        pT = sb("pT", [P, HG, P])
        rs0 = sb("rs0", [P, H])
        ctx0 = sb("ctx0", [P, KC * P])
        ctxT = sb("ctxT", [P, KC, P])

        pq = sb("pq", [P, H, H, HD])
        s1 = sb("s1", [P, H, H])
        mx1 = sb("mx1", [P, H])
        e1 = sb("e1", [P, H, H])
        rs1 = sb("rs1", [P, H])
        ri1 = sb("ri1", [P, H])
        pa = sb("pa", [P, H, HD, H])
        o1 = sb("o1", [P, H, HD])
        ctx1 = sb("ctx1", [P, HD, 32])
        y1 = sb("y1", [P, 2, 160])
        y2 = sb("y2", [P, 5, 64])

        bank_a = pb("bank_a")
        bank_s = ctx.enter_context(nc.psum_tensor("bank_s", [P, 2, 512], F32))
        bank_b = pb("bank_b")
        bank_c = pb("bank_c")
        bank_e = pb("bank_e")
        bank_f = pb("bank_f")
        bank_g = pb("bank_g")

        load = {n: sem("load_" + n) for n in (
            "c", "kmask", "wa0", "ba0", "wa1", "x0", "x", "qk", "v", "p0", "up0", "dn0", "qkv1", "wp1", "up1", "dn1")}
        S = {}
        for n in (
                "cleared built ones act_c dve_c1 dve_c2 dve_c pe_cT act_cT pe_mod0 pe_mod1 pe_mod2 pe_mod3 "
                "act_mod0 act_mod1 act_mod2 act_mod3 split0 split1 rest_ones borders zeros_qkv zeros_behind zeros_up padded w2half "
                "zeroed order_pe order_dve "
                "pe_rep0 pe_rep1 pe_rep2 pe_rep3 act_rep0 act_rep1 act_rep2 act_rep3 "
                "stats0 stats1 stats2 stats3 var0 var1 var2 var3 pool_ve0 pool_ve1 pool_ve2 pool_ve3 "
                "rstd0 rstd1 rstd2 rstd3 cen0 cen1 cen2 cen3 xm0 xm1 xm2 xm3 "
                "pe_xT0 pe_xT1 pe_xT2 pe_xT3 act_xT0 act_xT1 act_xT2 act_xT3 "
                "pe_v act_v pe_qk act_q act_k pe_s dve_mx dve_s act_p "
                "pe_pT act_pT pe_av dve_rs dve_ctx pe_cxT act_cxT pe_pr0 dve_g0 dve_x0 "
                "pe_up0 act_th dve_h pe_dn0 dve_g1 dve_x1 "
                "pe_qkv act_qkv dve_mx1 dve_e1 act_p1 dve_sum1 dve_ri1 dve_ctx1 dve_y1 dve_y2 pe_pr1 dve_g2 dve_x2 "
                "pe_up1 act_h1 pe_dn1 dve_g3 dve_x3 out "
                "pool_pq dve_s1 pool_pa dve_o1").split():
            S[n] = sem(n)

        def tile(ap, t):
            return ap[:, bass.ds(t, 1), :].rearrange("p a f -> p (a f)")

        def mod(t, k):
            return MOD[:, bass.ds(t, 1), k, :].rearrange("p a f -> p (a f)")

        def row(ap):
            return ap.rearrange("(a n) -> a n", a=1)

        def chunks(ap, p):
            return ap.rearrange("(k p) n -> p k n", p=p)

        def first(t):
            return isinstance(t, int) and t == 0

        def pipeline(engine, turn):
            for i in range(LOOP_FROM):
                turn(i, lambda lag, i=i: 0 <= i - lag < TILES)
            with engine.Fori(LOOP_FROM, TILES) as i:
                turn(i, lambda lag: True)
            for i in range(TILES, TILES + MAX_LAG):
                turn(i, lambda lag, i=i: 0 <= i - lag < TILES)

        def load_weights(engine, dst, src, bias, done, zeros):
            engine.dma_start(dst[1:P, 0, :], src[0:P - 1, :]).then_inc(load[done], 16)
            if bias is not None:
                engine.dma_start(dst[0:1, 0, :], row(bias)).then_inc(load[done], 16)
            engine.wait_ge(S[zeros[0]], zeros[1])
            engine.dma_start(dst[0:REST, 1, :], src[P - 1:D, :]).then_inc(load[done], 16)

        block = ctx.enter_context(nc.Block())

        @block.sync
        def _(sp):
            x_t = x.rearrange("b s f -> (b s) f").rearrange("(t p) f -> p t f", p=P)
            out_t = out.rearrange("b s f -> (b s) f").rearrange("(t p) f -> p t f", p=P)
            sp.dma_start(cnd[:], cond).then_inc(load["c"], 16)
            sp.dma_start(wa[0][0:KP], chunks(w["L0_cond_Wa"], KP)).then_inc(load["wa0"], 16)
            sp.dma_start(X[:, 0, :], x_t[:, 0, :]).then_inc(load["x0"], 16)
            load_weights(sp, wv, w["L0_cond_Wv"], None, "v", ("zeros_qkv", 1))
            sp.dma_start(X[:, 1:TILES, :], x_t[:, 1:TILES, :]).then_inc(load["x"], 16)
            load_weights(sp, w1[0], w["L0_cond_W1"], w["L0_cond_b1"], "up0", ("zeros_up", 1))
            for i, a, b in ((0, "L0_cond_W2", "L0_cond_b2"), (1, "L1_cond_fc2_w", "L1_cond_fc2_b")):
                full = (MC - 1) * P
                sp.dma_start(w2[i][:, 0:MC - 1, :], chunks(w[a][0:full], P)).then_inc(load[f"dn{i}"], 16)
                sp.dma_start(w2[i][0:ML, MC - 1, :], w[a][full:MLP]).then_inc(load[f"dn{i}"], 16)
                sp.dma_start(w2[i][ML:ML + 1, MC - 1, :], row(w[b])).then_inc(load[f"dn{i}"], 16)
            by_d = w["L1_cond_proj_w"].rearrange("(l d) n -> l d n", d=HD)
            for s in range(SEQS):
                for odd in range(2):
                    at = 32 * s + 16 * odd
                    sp.dma_start(wp1[at:at + 16, 0:5 - odd, :], by_d[:, odd:HD:2, :]).then_inc(load["wp1"], 16)
                sp.dma_start(wp1[32 * s + 16:32 * s + 17, 4, :], row(w["L1_cond_proj_b"])).then_inc(load["wp1"], 16)
            load_weights(sp, w1[1], w["L1_cond_fc1_w"], w["L1_cond_fc1_b"], "up1", ("zeros_up", 2))

            with sp.Fori(0, TILES) as t:
                sp.wait_ge(S["dve_x3"], t + 1)
                sp.dma_start(out_t[:, bass.ds(t, 1), :], X[:, bass.ds(t, 1), :]).then_inc(S["out"], 16)
            sp.wait_ge(S["out"], 16 * TILES)

        @block.gpsimd
        def _(pool):
            nc.gpsimd.memset(ident[:], 0.0).then_inc(S["cleared"], 1)
            nc.gpsimd.memset(tileb[:], 0.0).then_inc(S["cleared"], 1)
            nc.gpsimd.memset(selb[:], 0.0).then_inc(S["cleared"], 1)
            nc.gpsimd.memset(causalb[:], 0.0).then_inc(S["cleared"], 1)
            for i in LN:
                nc.gpsimd.memset(xm[i][:, 0:1], 1.0)
                nc.gpsimd.memset(xm[i][:, 1 + D:KC * P], 0.0)
            nc.gpsimd.memset(ctx0[:, 0:1], 1.0)
            nc.gpsimd.memset(ctx0[:, 1 + D:KC * P], 0.0).then_inc(S["borders"], 1)
            pool.wait_ge(S["cleared"], 4)

            def fill(ap, keep, value, base, pattern):
                return nc.gpsimd.affine_select(out=ap, in_=ap, compare_op=keep, fill=value, base=base,
                                               pattern=pattern, channel_multiplier=1)

            fill(ident[:], ALU.not_equal, 1.0, 0, [[-1, P]]).then_inc(S["built"], 1)
            for s in range(3):
                fill(tileb[:], ALU.not_equal, 1.0, -32 * s, [[-SEQS, TILES], [-1, SEQS], [0, SEQ]]).then_inc(S["built"], 1)
                pool.wait_ge(S["built"], s + 2)
            nc.gpsimd.memset(wp0[:, 1, :], 0.0)
            nc.gpsimd.memset(wqkv[:, 1, :], 0.0).then_inc(S["zeros_behind"], 1)
            nc.gpsimd.memset(w1[0][:, 1, :], 0.0).then_inc(S["zeros_up"], 1)
            nc.gpsimd.memset(w1[1][:, 1, :], 0.0).then_inc(S["zeros_up"], 1)
            fill(selb[:], ALU.not_equal, 1.0, 0, [[0, SEQS], [-1, SEQ]]).then_inc(S["built"], 1)
            fill(causalb[:], ALU.is_ge, MASKED, 0, [[0, 8], [-1, SEQ]]).then_inc(S["built"], 1)

            def rest_of_setup():
                for ap in (ctx1, y1):
                    last = nc.gpsimd.memset(ap[:], 0.0)
                last.then_inc(S["cleared"], 1)
                pool.wait_ge(S["cleared"], 5)
                nc.gpsimd.memset(hT[0][ML:ML + 1, MC - 1, :], 1.0)
                nc.gpsimd.memset(hT[1][ML:ML + 1, MC - 1, :], 1.0).then_inc(S["cleared"], 1)
                pool.wait_ge(S["cleared"], 6)
                nc.gpsimd.memset(y1[:, :, D:D + 1], 1.0).then_inc(S["rest_ones"], 1)

            def inverse_root(t, i):
                pool.wait_ge(S[f"var{i}"], t + 1)
                nc.gpsimd.tensor_tensor(ve[i][:], mv[i][:, 1:2], epst[:], ALU.add).then_inc(S[f"pool_ve{i}"], 1)
                pool.wait_ge(S[f"pool_ve{i}"], t + 1)
                nc.gpsimd.tensor_tensor(rstd[i][:], ve[i][:], mhalf[:], ALU.pow).then_inc(S[f"rstd{i}"], 1)

            def score_products(t, piece):
                hs = slice(piece * HG, (piece + 1) * HG)
                pool.wait_ge(S["act_qkv"], t + 1)
                q = tile(QKV, t)[:, 0:D].rearrange("p (h d) -> p h d", d=HD)[:, hs, :]
                k = tile(QKV, t)[:, D:2 * D].rearrange("p (h d) -> p h d", d=HD)
                nc.gpsimd.tensor_tensor(pq[:, hs], q.unsqueeze(2).broadcast_to([P, HG, H, HD]),
                                        k.unsqueeze(1).broadcast_to([P, HG, H, HD]), ALU.mult).then_inc(S["pool_pq"], 1)

            def value_products(t, piece):
                hs = slice(piece * HG, (piece + 1) * HG)
                pool.wait_ge(S["act_p1"], t + 1)
                p = tile(P1, t).rearrange("p (h k) -> p h k", k=H)[:, hs, :]
                v = tile(QKV, t)[:, 2 * D:3 * D].rearrange("p (h d) -> p d h", d=HD)
                nc.gpsimd.tensor_tensor(pa[:, hs], p.unsqueeze(2).broadcast_to([P, HG, HD, H]),
                                        v.unsqueeze(1).broadcast_to([P, HG, HD, H]), ALU.mult).then_inc(S["pool_pa"], 1)

            def turn(i, have):
                if have(0):
                    t = i
                    inverse_root(t, 0)
                if isinstance(i, int) and i == 0:
                    rest_of_setup()
                if have(5):
                    t = i - 5
                    inverse_root(t, 3)
                if have(2):
                    t = i - 2
                    inverse_root(t, 1)
                if have(3):
                    t = i - 3
                    score_products(t, 0)
                    score_products(t, 1)
                    score_products(t, 2)
                    score_products(t, 3)
                if have(4):
                    t = i - 4
                    value_products(t, 3)
                if have(3):
                    t = i - 3
                    value_products(t, 0)
                if have(2):
                    t = i - 2
                    inverse_root(t, 2)
                if have(3):
                    t = i - 3
                    value_products(t, 1)
                    value_products(t, 2)
            pipeline(pool, turn)

        @block.scalar
        def _(act):
            act.dma_start(kmask[:], heads).then_inc(load["kmask"], 16)
            act.dma_start(wa[0][KP:KP + 1, 0, :], row(w["L0_cond_ba"])).then_inc(load["ba0"], 16)
            load_weights(act, wqk0[:, :, 0, :], w["L0_cond_Wq"], None, "qk", ("zeros_qkv", 1))
            load_weights(act, wqk0[:, :, 1, :], w["L0_cond_Wk"], None, "qk", ("zeros_qkv", 1))
            act.dma_start(wa[1][0:KP], chunks(w["L1_cond_ada_w"], KP)).then_inc(load["wa1"], 16)
            act.dma_start(wa[1][KP:KP + 1, 0, :], row(w["L1_cond_ada_b"])).then_inc(load["wa1"], 16)
            act.wait_ge(load["c"], 16)
            nc.scalar.activation(cth[:], cnd[:], ACT.Tanh, scale=0.5).then_inc(S["act_c"], 1)
            load_weights(act, wp0, w["L0_cond_Wp"], w["L0_cond_bp"], "p0", ("zeros_behind", 1))
            act.wait_ge(S["pe_cT"], 1)
            act.wait_ge(S["ones"], 1)
            nc.scalar.activation(cT[0:KP], bank_a[0:KP, 0:KC * NSEQ].rearrange("p (k b) -> p k b", k=KC).unsqueeze(2)
                                 .broadcast_to([KP, KC, 3, NSEQ]), ACT.Copy).then_inc(S["act_cT"], 1)
            load_weights(act, wqkv, w["L1_cond_qkv_w"], w["L1_cond_qkv_b"], "qkv1", ("zeros_behind", 1))

            def modulation(q):
                act.wait_ge(S[f"pe_mod{q}"], 1)
                for k in range(3):
                    nc.scalar.activation(mods[q // 2][:, (3 * (q % 2) + k) * D:(3 * (q % 2) + k + 1) * D],
                                         (bank_b, bank_c, bank_f, bank_g)[q][0:96, k * D:(k + 1) * D],
                                         ACT.Copy, bias=1.0 if k == SCALE_A else 0.0).then_inc(S[f"act_mod{q}"], 1)

            for q in range(4):
                modulation(q)

            def copy_replicated(t, q):
                act.wait_ge(S[f"pe_rep{q}"], t + 1)
                nc.scalar.activation(MOD[:, bass.ds(t, 1), 3 * q:3 * q + 3, :].rearrange("p a k f -> p (a k f)"),
                                     bank_e[:, 0:3 * D], ACT.Copy).then_inc(S[f"act_rep{q}"], 1)

            def copy_norm(t, i):
                ps = (bank_a, bank_b, bank_e, bank_f)[i]
                act.wait_ge(S[f"pe_xT{i}"], t + 1)
                nc.scalar.activation(xmT[i][:].rearrange("p k t -> p (k t)"), ps[:, 0:KC * P], ACT.Copy
                                     ).then_inc(S[f"act_xT{i}"], 1)

            def spread_values(t):
                if first(t):
                    act.wait_ge(S["ones"], 2)
                if not first(t):
                    act.wait_ge(S["pe_av"], t)
                act.wait_ge(S["pe_v"], t + 1)
                for h in range(HG):
                    r = slice(32 * h, 32 * h + 32)
                    last = nc.scalar.activation(Vx[r, :, :, h, 0:HD].rearrange("p b g d -> p (b g) d"),
                                                bank_s[r, 0, 0:D].rearrange("p (a d) -> p a d", d=HD), ACT.Copy)
                last.then_inc(S["act_v"], 1)

            def copy_queries(t):
                act.wait_ge(S["pe_qk"], t + 1)
                nc.scalar.activation(qT[:].rearrange("p j t -> p (j t)"), bank_a[0:HI + GW, 0:2 * P], ACT.Copy
                                     ).then_inc(S["act_q"], 1)

            def spread_keys(t):
                if first(t):
                    act.wait_ge(load["kmask"], 16)
                act.wait_ge(S["pe_qk"], t + 1)
                for h in range(HG):
                    last = nc.scalar.activation(
                        Kx[:, :, :, h, :].rearrange("p j b k -> p (j b) k"),
                        bank_a[0:HI + GW, 2 * P:4 * P].rearrange("p (a k) -> p a k", k=SEQ), ACT.Copy,
                        scale=kmask[:, h:h + 1])
                last.then_inc(S["act_k"], 1)

            def exp_causal(t):
                act.wait_ge(S["dve_s"], t + 1)
                nc.scalar.activation(p0[:], s0[:], ACT.Exp, scale=SCALE).then_inc(S["act_p"], 1)

            def copy_probs(t):
                act.wait_ge(S["pe_pT"], t + 1)
                nc.scalar.activation(pT[:].rearrange("p g t -> p (g t)"), bank_b[:], ACT.Copy).then_inc(S["act_pT"], 1)

            def copy_context(t):
                act.wait_ge(S["pe_cxT"], t + 1)
                nc.scalar.activation(ctxT[:].rearrange("p k t -> p (k t)"), bank_b[:, 0:KC * P], ACT.Copy
                                     ).then_inc(S["act_cxT"], 1)

            def tanh_hidden(t):
                act.wait_ge(S["pe_up0"], t + 1)
                nc.scalar.activation(th[:, 0:MC - 1, :].rearrange("p m t -> p (m t)"), bank_b[:], ACT.Tanh, scale=0.5)
                nc.scalar.activation(th[0:ML, MC - 1, :], bank_c[0:ML, 0:P], ACT.Tanh, scale=0.5).then_inc(S["act_th"], 1)

            def copy_qkv(t):
                act.wait_ge(S["pe_qkv"], t + 1)
                nc.scalar.activation(tile(QKV, t), bank_e[:, 0:3 * D], ACT.Copy).then_inc(S["act_qkv"], 1)

            def exp_heads(t):
                act.wait_ge(S["dve_e1"], t + 1)
                nc.scalar.activation(tile(P1, t), e1[:].rearrange("p h k -> p (h k)"), ACT.Exp, scale=SCALE
                                     ).then_inc(S["act_p1"], 1)

            def gelu_hidden(t):
                act.wait_ge(S["pe_up1"], t + 1)
                nc.scalar.activation(hT[1][:, 0:MC - 1, :].rearrange("p m t -> p (m t)"), bank_f[:], ACT.Gelu)
                nc.scalar.activation(hT[1][0:ML, MC - 1, :], bank_g[0:ML, 0:P], ACT.Gelu).then_inc(S["act_h1"], 1)

            def turn(i, have):
                if have(2):
                    t = i - 2
                    copy_replicated(t, 2)
                if have(6):
                    t = i - 6
                    copy_norm(t, 3)
                if have(1):
                    t = i - 1
                    copy_norm(t, 0)
                if have(3):
                    t = i - 3
                    tanh_hidden(t)
                if have(2):
                    t = i - 2
                    exp_causal(t)
                if have(0):
                    t = i
                    copy_replicated(t, 0)
                if have(6):
                    t = i - 6
                    gelu_hidden(t)
                if have(4):
                    t = i - 4
                    exp_heads(t)
                if have(2):
                    t = i - 2
                    copy_probs(t)
                if have(1):
                    t = i - 1
                    copy_queries(t)
                if have(0):
                    t = i
                    copy_replicated(t, 1)
                if have(2):
                    t = i - 2
                    copy_replicated(t, 3)
                    copy_context(t)
                if have(3):
                    t = i - 3
                    copy_norm(t, 2)
                if have(1):
                    t = i - 1
                    spread_keys(t)
                    spread_values(t)
                if have(3):
                    t = i - 3
                    copy_qkv(t)
                if have(2):
                    t = i - 2
                    copy_norm(t, 1)
            pipeline(act, turn)

        @block.vector
        def _(dve):
            nc.vector.memset(cT[:], 1.0).then_inc(S["ones"], 1)
            nc.vector.memset(epst[:], EPS)
            nc.vector.memset(mhalf[:], -0.5)
            nc.vector.memset(wqk0[:, 1, :, :], 0.0)
            nc.vector.memset(wqk0[0:1, 0, :, :], 0.0)
            nc.vector.memset(wv[0:1, 0, :], 0.0)
            nc.vector.memset(wv[:, 1, :], 0.0).then_inc(S["zeros_qkv"], 1)
            dve.wait_ge(S["act_c"], 1)
            nc.vector.tensor_tensor(cgt[:], cth[:], cnd[:], ALU.mult).then_inc(S["dve_c1"], 1)
            dve.wait_ge(S["dve_c1"], 1)
            nc.vector.tensor_tensor(cth[:], cgt[:], cnd[:], ALU.add).then_inc(S["dve_c2"], 1)
            dve.wait_ge(S["dve_c2"], 1)
            nc.vector.tensor_scalar_mul(csl[:], cth[:], 0.5).then_inc(S["dve_c"], 1)
            nc.vector.memset(Vx[:], 0.0).then_inc(S["zeroed"], 1)
            dve.wait_ge(S["zeroed"], 1)
            for h in range(HG):
                last = nc.vector.memset(Vx[32 * h:32 * h + 32, :, :, h, HD:HD + 1], 1.0)
            last.then_inc(S["ones"], 1)
            nc.vector.memset(wqk[:], 0.0).then_inc(S["zeroed"], 1)
            dve.wait_ge(load["qk"], 4 * 16)
            dve.wait_ge(S["zeroed"], 2)
            for which in range(2):
                for r, at in enumerate((LO, HI)):
                    last = nc.vector.tensor_copy(wqk[:, :, which, :, at:at + GW],
                                                 wqk0[:, :, which, :].rearrange("p k (j r c) -> p k j r c", j=2, r=2)[:, :, :, r, :])
            last.then_inc(S["padded"], 1)

            def split_modulation(layer):
                low = slice(64, 96)
                done = S[f"split{layer}"]
                step = 0
                for half in range(2):
                    c = slice(half * 3 * D, (half + 1) * 3 * D)
                    dve.wait_ge(S[f"act_mod{2 * layer + half}"], 3)
                    for out_, a, b in ((stack[layer][:, c], mods[layer][:, c], None),
                                       (rest[:, c], mods[layer][:, c], stack[layer][:, c]),
                                       (stack[layer][32:64, c], rest[32:64, c], None),
                                       (midb[low, c], rest[low, c], None),
                                       (rest[low, c], rest[low, c], midb[low, c]),
                                       (stack[layer][low, c], rest[low, c], None)):
                        if b is None:
                            last = nc.vector.tensor_copy(out_, a)
                        else:
                            last = nc.vector.tensor_tensor(out_, a, b, ALU.subtract)
                        last.then_inc(done, 1)
                        step += 1
                        dve.wait_ge(done, step)

            split_modulation(0)

            def halve_w2():
                dve.wait_ge(load["dn0"], 3 * 16)
                nc.vector.tensor_scalar_mul(w2[0][:, 0:MC - 1, :], w2[0][:, 0:MC - 1, :], 0.5)
                nc.vector.tensor_scalar_mul(w2[0][0:ML, MC - 1, :], w2[0][0:ML, MC - 1, :], 0.5).then_inc(S["w2half"], 1)

            def statistics(t, i):
                if isinstance(t, int) and i == 0 and t < 2:
                    dve.wait_ge(load[("x0", "x")[t]], 16)
                    dve.sem_inc(S["order_dve"], 1)
                if i:
                    dve.wait_ge(S[f"dve_x{i - 1}"], t + 1)
                    dve.sem_inc(S["order_dve"], 1)
                nc.vector.bn_stats(st[i][:], tile(X, t)).then_inc(S[f"stats{i}"], 1)

            def variance(t, i):
                dve.wait_ge(S[f"stats{i}"], t + 1)
                dve.sem_inc(S["order_dve"], 1)
                nc.vector.bn_aggr(mv[i][:], st[i][:]).then_inc(S[f"var{i}"], 1)

            def centre(t, i):
                q = i
                dve.wait_ge(S[f"act_rep{q}"], t + 1)
                dve.wait_ge(S[f"var{i}"], t + 1)
                nc.vector.scalar_tensor_tensor(u[i][:], tile(X, t), mv[i][:, 0:1], mod(t, 3 * i + 1), ALU.subtract, ALU.mult
                                               ).then_inc(S[f"cen{i}"], 1)

            def modulate(t, i):
                dve.wait_ge(S[f"rstd{i}"], t + 1)
                dve.wait_ge(S[f"cen{i}"], t + 1)
                nc.vector.scalar_tensor_tensor(xm[i][:, 1:1 + D], u[i][:], rstd[i][:], mod(t, 3 * i), ALU.mult, ALU.add
                                               ).then_inc(S[f"xm{i}"], 1)

            def gate(t, i):
                done = ("pe_pr0", "pe_dn0", "pe_pr1", "pe_dn1")[i]
                ps = (bank_c, bank_e, bank_g, bank_g)[i]
                at = 2 * P if i == 3 else 0
                if i == 3 and not first(t):
                    dve.wait_ge(S["dve_x3"], t)
                dve.wait_ge(S[done], t + 1)
                nc.vector.tensor_tensor(g[i][:], ps[:, at:at + D], mod(t, 3 * i + 2), ALU.mult).then_inc(S[f"dve_g{i}"], 1)

            def residual(t, i):
                dve.wait_ge(S[f"dve_g{i}"], t + 1)
                nc.vector.tensor_tensor(tile(X, t), tile(X, t), g[i][:], ALU.add).then_inc(S[f"dve_x{i}"], 1)

            scores = bank_s[:, :, 0:8 * SEQ].rearrange("p r (h k) -> p r h k", k=SEQ)

            def causal_max(t):
                dve.wait_ge(S["pe_s"], t + 1)
                nc.vector.tensor_reduce(mx0[:], scores, axis=AX.X, op=ALU.max).then_inc(S["dve_mx"], 1)

            def causal_shift(t):
                dve.wait_ge(S["dve_mx"], t + 1)
                nc.vector.tensor_tensor(s0[:], scores, mx0[:].unsqueeze(3).broadcast_to([P, 2, 8, SEQ]), ALU.subtract
                                        ).then_inc(S["dve_s"], 1)

            weighted = bank_c[:, 0:H * (HD + 1)].rearrange("p (h e) -> p h e", e=HD + 1)

            def causal_sum_inverse(t):
                dve.wait_ge(S["pe_av"], t + 1)
                nc.vector.reciprocal(rs0[:].unsqueeze(2), weighted[:, :, HD:HD + 1]).then_inc(S["dve_rs"], 1)

            def causal_context(t):
                dve.wait_ge(S["dve_rs"], t + 1)
                nc.vector.tensor_tensor(ctx0[:, 1:1 + D].rearrange("p (h d) -> p h d", d=HD), weighted[:, :, 0:HD],
                                        rs0[:].unsqueeze(2).broadcast_to([P, H, HD]), ALU.mult).then_inc(S["dve_ctx"], 1)

            def silu_hidden(t):
                dve.wait_ge(S["act_th"], t + 1)
                nc.vector.scalar_tensor_tensor(hT[0][:, 0:MC - 1, :].rearrange("p m t -> p (m t)"),
                                               th[:, 0:MC - 1, :].rearrange("p m t -> p (m t)"), 1.0, bank_b[:],
                                               ALU.add, ALU.mult)
                nc.vector.scalar_tensor_tensor(hT[0][0:ML, MC - 1, :], th[0:ML, MC - 1, :], 1.0, bank_c[0:ML, 0:P],
                                               ALU.add, ALU.mult).then_inc(S["dve_h"], 1)

            def sum_scores(t, piece):
                hs = slice(piece * HG, (piece + 1) * HG)
                dve.wait_ge(S["pool_pq"], t * HG + piece + 1)
                nc.vector.tensor_reduce(s1[:, hs], pq[:, hs], axis=AX.X, op=ALU.add).then_inc(S["dve_s1"], 1)

            def heads_max(t):
                dve.wait_ge(S["dve_s1"], t * HG + HG)
                nc.vector.tensor_reduce(mx1[:], s1[:], axis=AX.X, op=ALU.max).then_inc(S["dve_mx1"], 1)

            def heads_shift(t):
                dve.wait_ge(S["dve_mx1"], t + 1)
                nc.vector.tensor_tensor(e1[:], s1[:], mx1[:].unsqueeze(2).broadcast_to([P, H, H]), ALU.subtract
                                        ).then_inc(S["dve_e1"], 1)

            def heads_sum(t):
                dve.wait_ge(S["act_p1"], t + 1)
                nc.vector.tensor_reduce(rs1[:], tile(P1, t).rearrange("p (h k) -> p h k", k=H), axis=AX.X, op=ALU.add
                                        ).then_inc(S["dve_sum1"], 1)

            def heads_sum_inverse(t):
                dve.wait_ge(S["dve_sum1"], t + 1)
                nc.vector.reciprocal(ri1[:], rs1[:]).then_inc(S["dve_ri1"], 1)

            def sum_values(t, piece):
                hs = slice(piece * HG, (piece + 1) * HG)
                dve.wait_ge(S["pool_pa"], t * HG + piece + 1)
                nc.vector.tensor_reduce(o1[:, hs], pa[:, hs], axis=AX.X, op=ALU.add).then_inc(S["dve_o1"], 1)

            def heads_context(t):
                dve.wait_ge(S["dve_ri1"], t + 1)
                dve.wait_ge(S["dve_o1"], t * HG + HG)
                nc.vector.tensor_tensor(ctx1[:, :, 0:H].rearrange("p d h -> p h d"), o1[:],
                                        ri1[:].unsqueeze(2).broadcast_to([P, H, HD]), ALU.mult).then_inc(S["dve_ctx1"], 1)

            def heads_to_rows(t):
                dve.wait_ge(S["dve_ctx1"], t + 1)
                nc.vector.transpose(y1[:, :, 0:D].rearrange("p a (d l) -> p d a l", l=16), ctx1[:]).then_inc(S["dve_y1"], 1)

            def features_to_rows(t):
                dve.wait_ge(S["dve_y1"], t + 1)
                nc.vector.transpose(y2[:].rearrange("p j (c a) -> p a j c", a=2),
                                    y1[:].rearrange("p a (j x) -> p a j x", x=32)).then_inc(S["dve_y2"], 1)

            def turn(i, have):
                if have(0):
                    t = i
                    statistics(t, 0)
                    variance(t, 0)
                if have(2):
                    t = i - 2
                    gate(t, 0)
                if have(5):
                    t = i - 5
                    variance(t, 3)
                if have(2):
                    t = i - 2
                    residual(t, 0)
                    statistics(t, 1)
                    variance(t, 1)
                if have(0):
                    t = i
                    centre(t, 0)
                if have(2):
                    t = i - 2
                    centre(t, 1)
                if have(5):
                    t = i - 5
                    centre(t, 3)
                if have(0):
                    t = i
                    modulate(t, 0)
                if isinstance(i, int) and i == 0:
                    split_modulation(1)
                    halve_w2()
                if have(2):
                    t = i - 2
                    modulate(t, 1)
                if have(5):
                    t = i - 5
                    modulate(t, 3)
                if have(4):
                    t = i - 4
                    sum_values(t, 1)
                if have(1):
                    t = i - 1
                    causal_max(t)
                if have(3):
                    t = i - 3
                    sum_scores(t, 0)
                if have(4):
                    t = i - 4
                    sum_values(t, 2)
                if have(3):
                    t = i - 3
                    sum_scores(t, 1)
                if have(1):
                    t = i - 1
                    causal_shift(t)
                if have(6):
                    t = i - 6
                    residual(t, 3)
                if have(3):
                    t = i - 3
                    sum_scores(t, 2)
                if have(2):
                    t = i - 2
                    silu_hidden(t)
                if have(3):
                    t = i - 3
                    sum_scores(t, 3)
                    heads_max(t)
                    heads_shift(t)
                if have(4):
                    t = i - 4
                    sum_values(t, 3)
                if have(2):
                    t = i - 2
                    gate(t, 1)
                if have(4):
                    t = i - 4
                    heads_context(t)
                if have(2):
                    t = i - 2
                    residual(t, 1)
                if have(4):
                    t = i - 4
                    heads_to_rows(t)
                    features_to_rows(t)
                if have(2):
                    t = i - 2
                    statistics(t, 2)
                if have(5):
                    t = i - 5
                    gate(t, 3)
                if have(2):
                    t = i - 2
                    variance(t, 2)
                    centre(t, 2)
                if have(1):
                    t = i - 1
                    causal_sum_inverse(t)
                if have(3):
                    t = i - 3
                    heads_sum(t)
                if have(1):
                    t = i - 1
                    causal_context(t)
                if have(2):
                    t = i - 2
                    modulate(t, 2)
                if have(3):
                    t = i - 3
                    heads_sum_inverse(t)
                    sum_values(t, 0)
                if have(4):
                    t = i - 4
                    gate(t, 2)
                    residual(t, 2)
                    statistics(t, 3)

            pipeline(dve, turn)

        @block.tensor
        def _(pe):
            mm = nc.tensor.matmul
            pe.wait_ge(S["built"], 1)
            pe.wait_ge(S["dve_c"], 1)
            for k in range(KC):
                last = nc.tensor.transpose(bank_a[0:KP, k * NSEQ:(k + 1) * NSEQ], csl[:, k * KP:(k + 1) * KP],
                                           ident[0:NSEQ, 0:NSEQ])
            last.then_inc(S["pe_cT"], 1)
            pe.wait_ge(S["act_cT"], 1)

            def modulation(q):
                for k in range(KC):
                    r = KP + 1 - k
                    last = mm((bank_b, bank_c, bank_f, bank_g)[q][0:96, 0:3 * D], cT[0:r, k, :],
                              wa[q // 2][0:r, k, q % 2 * 3 * D:(q % 2 + 1) * 3 * D], start=k == 0, stop=k == KC - 1)
                last.then_inc(S[f"pe_mod{q}"], 1)

            pe.wait_ge(load["wa0"], 16)
            pe.wait_ge(load["ba0"], 16)
            modulation(0)
            modulation(1)
            pe.wait_ge(load["wa1"], 2 * 16)
            modulation(2)
            modulation(3)

            def after_bank_e(i, have, readers):
                for signal, lag in readers:
                    if have(lag):
                        pe.wait_ge(S[signal], i - lag + 1)
                        return

            def replicate(t, q):
                if first(t):
                    pe.wait_ge(S[f"split{q // 2}"], 6 * (q % 2 + 1))
                    pe.wait_ge(S["built"], 4)
                mm(bank_e[:, 0:3 * D], tileb[:, bass.ds(t, 1)].rearrange("p a s q -> p (a s q)"),
                   stack[q // 2][:, q % 2 * 3 * D:(q % 2 + 1) * 3 * D], start=True, stop=True).then_inc(S[f"pe_rep{q}"], 1)

            def transpose_norm(t, i):
                ps = (bank_a, bank_b, bank_e, bank_f)[i]
                if i in (0, 3) and not first(t):
                    pe.wait_ge(S["act_k" if i == 0 else "act_h1"], t)
                if first(t):
                    pe.wait_ge(S["borders"], 1)
                pe.wait_ge(S[f"xm{i}"], t + 1)
                for k in range(KC):
                    last = nc.tensor.transpose(ps[:, k * P:(k + 1) * P], xm[i][:, k * P:(k + 1) * P], ident[:])
                last.then_inc(S[f"pe_xT{i}"], 1)

            def values(t):
                if first(t):
                    pe.wait_ge(load["v"], 2 * 16)
                if not first(t):
                    pe.wait_ge(S["dve_s"], t)
                pe.wait_ge(S["act_xT0"], t + 1)
                for b in range(SEQS):
                    for k in range(KC):
                        for h in range(HG):
                            last = mm(bank_s[32 * h:32 * h + 32, 0, b * GW:(b + 1) * GW],
                                      xmT[0][:, k, b * SEQ:(b + 1) * SEQ],
                                      wv[:, k, :].rearrange("p (g h d) -> p g h d", g=HG, h=HG)[:, :, h, :],
                                      start=k == 0, stop=k == KC - 1)
                last.then_inc(S["pe_v"], 1)

            def queries_keys(t):
                if first(t):
                    pe.wait_ge(S["padded"], 1)
                pe.wait_ge(S["act_xT0"], t + 1)
                for which in range(2):
                    for j in range(2):
                        col = (2 * which + j) * P
                        for k in range(KC):
                            last = mm(bank_a[0:HI + GW, col:col + P], wqk[:, k, which, j, :], xmT[0][:, k, :],
                                      start=k == 0, stop=k == KC - 1)
                last.then_inc(S["pe_qk"], 1)

            def causal_scores(t):
                if first(t):
                    pe.wait_ge(S["built"], 6)
                pe.wait_ge(S["act_v"], t + 1)
                pe.wait_ge(S["act_q"], t + 1)
                pe.wait_ge(S["act_k"], t + 1)
                for r in range(2):
                    mm(bank_s[:, r, 0:8 * SEQ], selb[:].rearrange("p s q -> p (s q)"),
                       causalb[:].rearrange("p h k -> p (h k)"), start=True, stop=False, skip_group_check=True)
                for j in range(2):
                    for b in range(SEQS):
                        for r, at in enumerate((LO, HI)):
                            last = mm(bank_s[32 * b:32 * b + 32, r, j * P:(j + 1) * P],
                                      qT[at:at + GW, j, b * SEQ:(b + 1) * SEQ],
                                      Kx[at:at + GW, j, b].rearrange("p h k -> p (h k)"),
                                      start=False, stop=True, skip_group_check=True)
                last.then_inc(S["pe_s"], 1)

            def transpose_probs(t):
                if not first(t):
                    pe.wait_ge(S["dve_h"], t)
                pe.wait_ge(S["act_p"], t + 1)
                for k in range(HG):
                    last = nc.tensor.transpose(bank_b[:, k * P:(k + 1) * P],
                                               p0[:, k // 2, k % 2 * HG:k % 2 * HG + HG, :].rearrange("p h k -> p (h k)"),
                                               ident[:])
                last.then_inc(S["pe_pT"], 1)

            def weigh_values(t):
                pe.wait_ge(S["act_pT"], t + 1)
                for k in range(HG):
                    group = k % 2 * 2 + k // 2
                    for b in range(SEQS):
                        last = mm(bank_c[32 * b:32 * b + 32, group * HG * (HD + 1):(group + 1) * HG * (HD + 1)],
                                  pT[:, k, b * SEQ:(b + 1) * SEQ], Vx[:, b, group].rearrange("p h e -> p (h e)"),
                                  start=True, stop=True)
                last.then_inc(S["pe_av"], 1)

            def transpose_context(t):
                pe.wait_ge(S["dve_ctx"], t + 1)
                for k in range(KC):
                    last = nc.tensor.transpose(bank_b[:, k * P:(k + 1) * P], ctx0[:, k * P:(k + 1) * P], ident[:])
                last.then_inc(S["pe_cxT"], 1)

            def project0(t):
                if first(t):
                    pe.wait_ge(load["p0"], 3 * 16)
                pe.wait_ge(S["act_cxT"], t + 1)
                for k in range(KC):
                    last = mm(bank_c[:, 0:D], ctxT[:, k, :], wp0[:, k, :], start=k == 0, stop=k == KC - 1)
                last.then_inc(S["pe_pr0"], 1)

            def hidden(t, i):
                if first(t):
                    pe.wait_ge(load[f"up{i}"], 3 * 16)
                xi, big, small = ((1, bank_b, bank_c), (3, bank_f, bank_g))[i]
                pe.wait_ge(S[f"act_xT{xi}"], t + 1)
                for m in range(MC):
                    cols = P if m < MC - 1 else ML
                    dst = big[:, m * P:(m + 1) * P] if m < MC - 1 else small[0:ML, 0:P]
                    for k in range(KC):
                        last = mm(dst, w1[i][:, k, m * P:m * P + cols], xmT[xi][:, k, :],
                                  start=k == 0, stop=k == KC - 1)
                last.then_inc(S[f"pe_up{i}"], 1)

            def mlp_out(t, i):
                if first(t):
                    pe.wait_ge(load[f"dn{i}"], 3 * 16)
                    if i == 0:
                        pe.wait_ge(S["w2half"], 1)
                dst = (bank_e[:, 0:D], bank_g[:, 2 * P:2 * P + D])[i]
                pe.wait_ge(S[("dve_h", "act_h1")[i]], t + 1)
                for m in range(MC):
                    r = P if m < MC - 1 else ML + 1
                    last = mm(dst, hT[i][0:r, m, :], w2[i][0:r, m, :], start=m == 0, stop=m == MC - 1)
                last.then_inc(S[f"pe_dn{i}"], 1)

            def qkv1(t):
                if first(t):
                    pe.wait_ge(load["qkv1"], 3 * 16)
                pe.wait_ge(S["act_xT2"], t + 1)
                for k in range(KC):
                    last = mm(bank_e[:, 0:3 * D], xmT[2][:, k, :], wqkv[:, k, :], start=k == 0, stop=k == KC - 1)
                last.then_inc(S["pe_qkv"], 1)

            def project1(t):
                if first(t):
                    pe.wait_ge(load["wp1"], 3 * SEQS * 16)
                if not first(t):
                    pe.wait_ge(S["dve_g3"], t)
                pe.wait_ge(S["dve_y2"], t + 1)
                pe.sem_inc(S["order_pe"], 1)
                for j in range(5):
                    rows = 32 if j < 4 else 17
                    for s in range(SEQS):
                        last = mm(bank_g[32 * s:32 * s + 32, 0:D], y2[32 * s:32 * s + rows, j, 0:SEQ],
                                  wp1[32 * s:32 * s + rows, j, :], start=j == 0, stop=j == 4)
                last.then_inc(S["pe_pr1"], 1)

            def turn(i, have):
                if have(0):
                    t = i
                    after_bank_e(i, have, (("act_rep2", 2), ("act_qkv", 4), ("act_rep3", 3), ("act_rep1", 1), ("dve_g1", 4), ("act_rep0", 1)))
                    replicate(t, 0)
                if have(6):
                    t = i - 6
                    hidden(t, 1)
                if have(1):
                    t = i - 1
                    queries_keys(t)
                if have(2):
                    t = i - 2
                    transpose_probs(t)
                if have(3):
                    t = i - 3
                    after_bank_e(i, have, (("act_rep0", 0), ("act_rep2", 2), ("act_qkv", 4), ("act_rep3", 3), ("act_rep1", 1), ("dve_g1", 4)))
                    mlp_out(t, 0)
                if have(6):
                    t = i - 6
                    mlp_out(t, 1)
                if have(0):
                    t = i
                    after_bank_e(i, have, (("dve_g1", 3), ("act_rep0", 0), ("act_rep2", 2), ("act_qkv", 4), ("act_rep3", 3), ("act_rep1", 1)))
                    replicate(t, 1)
                if have(2):
                    t = i - 2
                    weigh_values(t)
                    after_bank_e(i, have, (("act_rep1", 0), ("dve_g1", 3), ("act_rep0", 0), ("act_rep2", 2), ("act_qkv", 4), ("act_rep3", 3)))
                    replicate(t, 3)
                if have(5):
                    t = i - 5
                    project1(t)
                if have(2):
                    t = i - 2
                    transpose_context(t)
                if have(3):
                    t = i - 3
                    after_bank_e(i, have, (("act_rep3", 2), ("act_rep1", 0), ("dve_g1", 3), ("act_rep0", 0), ("act_rep2", 2), ("act_qkv", 4)))
                    transpose_norm(t, 2)
                if have(1):
                    t = i - 1
                    values(t)
                if have(2):
                    t = i - 2
                    project0(t)
                if have(3):
                    t = i - 3
                    qkv1(t)
                if have(1):
                    t = i - 1
                    causal_scores(t)
                if have(2):
                    t = i - 2
                    transpose_norm(t, 1)
                if have(1):
                    t = i - 1
                    after_bank_e(i, have, (("act_qkv", 3), ("act_rep3", 2), ("act_rep1", 0), ("dve_g1", 3), ("act_rep0", 0), ("act_rep2", 2)))
                    replicate(t, 2)
                if have(5):
                    t = i - 5
                    transpose_norm(t, 3)
                if have(0):
                    t = i
                    transpose_norm(t, 0)
                if have(2):
                    t = i - 2
                    hidden(t, 0)
            pipeline(pe, turn)


_W = ['L0_cond_Wq', 'L0_cond_Wk', 'L0_cond_Wv', 'L0_cond_Wp', 'L0_cond_bp', 'L0_cond_W1', 'L0_cond_b1', 'L0_cond_W2',
      'L0_cond_b2', 'L0_cond_Wa', 'L0_cond_ba', 'L1_cond_qkv_w', 'L1_cond_qkv_b', 'L1_cond_proj_w', 'L1_cond_proj_b',
      'L1_cond_fc1_w', 'L1_cond_fc1_b', 'L1_cond_fc2_w', 'L1_cond_fc2_b', 'L1_cond_ada_w', 'L1_cond_ada_b']


def kernel(**inputs):
    import numpy as _np
    import concourse.bacc as _bacc
    from concourse import mybir as _mybir
    from concourse.bass_utils import run_bass_kernel_spmd as _run

    nc = _bacc.Bacc("TRN2", target_bir_lowering=False, num_devices=1)
    arrays, aps = {}, {}
    for name in ['x', 'cond_1152', *_W]:
        a = _np.ascontiguousarray(inputs[name])
        arrays[f"in_{name}"] = a
        aps[name] = nc.dram_tensor(f"in_{name}", a.shape, _mybir.dt.from_np(a.dtype), kind="ExternalInput").ap()
    arrays["in_head_rows"] = head_rows()
    heads = nc.dram_tensor("in_head_rows", (HI + GW, HG), F32, kind="ExternalInput").ap()
    out = nc.dram_tensor("out", (NSEQ, SEQ, D), F32, kind="ExternalOutput").ap()
    build(nc, aps["x"], aps["cond_1152"], {n: aps[n] for n in _W}, heads, out)
    r = _run(nc, [arrays], core_ids=[0])
    return r.results[0]["out"]
```

```python
import concourse.bass as bass
from concourse import mybir
from contextlib import ExitStack

F32 = mybir.dt.float32
BF16 = mybir.dt.bfloat16
ALU = mybir.AluOpType
ACT = mybir.ActivationFunctionType
AX = mybir.AxisListType

NSEQ, SEQ, D = 32, 32, 144
H = 16
HD = D // H
P = 128
TILES = NSEQ * SEQ // P
SEQS = P // SEQ
KC = 2
KP = D // KC
HG = 4
GW = HG * HD
REST = D + 1 - P
MLP = 4 * D
MC = (MLP + P - 1) // P
ML = MLP - (MC - 1) * P
NMOD = 6
EPS = 1e-6
SCALE = 1.0 / 3.0
MASKED = -1e30
LO, HI = 0, 64
SCALE_A = 1
MAX_LAG = 6
POOL_PIECES = 3
WARMUP = 14
LOOP_FROM = 7



def head_rows():
    import numpy as np
    m = np.zeros((HI + GW, HG), np.float32)
    for r in range(GW):
        m[LO + r, r // HD] = m[HI + r, r // HD] = 1.0
    return m


def scale_ones():
    import numpy as np
    m = np.zeros((1, NMOD * D), np.float32)
    for half in range(2):
        at = (3 * half + SCALE_A) * D
        m[0, at:at + D] = 1.0
    return m


def build(nc, x, cond, w, heads, ones_of_scales, out):
    ctx = ExitStack()
    with ctx:
        def sb(name, shape, dt=F32):
            return ctx.enter_context(nc.sbuf_tensor(name, shape, dt))

        def pb(name):
            return ctx.enter_context(nc.psum_tensor(name, [P, 512], F32))

        def sem(name):
            return ctx.enter_context(nc.semaphore(name))

        X = sb("X", [P, TILES, D])
        MOD = sb("MOD", [P, TILES, 2 * NMOD, D])
        QKV = sb("QKV", [P, TILES, 3 * D])
        P1 = sb("P1", [P, TILES, H * H])
        ident = sb("ident", [P, P])
        kmask = sb("kmask", [HI + GW, HG])
        selb = sb("selb", [SEQ, SEQS, SEQ], BF16)
        causalb = sb("causalb", [SEQ, 8, SEQ], BF16)
        tileb = sb("tileb", [96, TILES, SEQS, SEQ], BF16)
        cnd = sb("cnd", [NSEQ, D])
        cth = sb("cth", [NSEQ, D])
        cgt = sb("cgt", [NSEQ, D])
        csl = sb("csl", [NSEQ, D])
        cT = sb("cT", [KP + 1, KC, 96])
        wa = [sb(f"wa{i}", [KP + 1, KC, NMOD * D]) for i in range(2)]
        rest = sb("rest", [96, 3 * D])
        midb = sb("midb", [96, 3 * D], BF16)
        warm = sb("warm", [P, 512], BF16)
        stack = [sb(f"stack{i}", [96, NMOD * D], BF16) for i in range(2)]

        wqk0 = sb("wqk0", [P, KC, 2, D])
        wqk = sb("wqk", [P, KC, 2, 2, HI + GW])
        wv = sb("wv", [P, KC, D])
        wp0 = sb("wp0", [P, KC, D])
        wqkv = sb("wqkv", [P, KC, 3 * D])
        wp1 = sb("wp1", [P, 5, D])
        w1 = [sb(f"w1_{i}", [P, KC, MLP]) for i in range(2)]
        w2 = [sb(f"w2_{i}", [P, MC, D]) for i in range(2)]

        epst = sb("epst", [P, 1])
        mhalf = sb("mhalf", [P, 1])
        LN = range(4)
        st = [sb(f"st{i}", [P, 6]) for i in LN]
        mv = [sb(f"mv{i}", [P, 2]) for i in LN]
        ve = [sb(f"ve{i}", [P, 1]) for i in LN]
        rstd = [sb(f"rstd{i}", [P, 1]) for i in LN]
        u = [sb(f"u{i}", [P, D]) for i in LN]
        xm = [sb(f"xm{i}", [P, KC * P]) for i in LN]
        xmT = [sb(f"xmT{i}", [P, KC, P]) for i in LN]
        g = [sb(f"g{i}", [P, D]) for i in range(4)]
        th = sb("th", [P, MC, P])
        hT = [sb(f"hT{i}", [P, MC, P]) for i in range(2)]

        qT = sb("qT", [HI + GW, 2, P])
        Kx = sb("Kx", [HI + GW, 2, SEQS, HG, SEQ])
        Vx = sb("Vx", [P, SEQS, HG, HG, HD + 1])
        mx0 = sb("mx0", [P, 2, 8])
        s0 = sb("s0", [P, 2, 8, SEQ])
        p0 = sb("p0", [P, 2, 8, SEQ])
        pT = sb("pT", [P, HG, P])
        rs0 = sb("rs0", [P, H])
        ctx0 = sb("ctx0", [P, KC * P])
        ctxT = sb("ctxT", [P, KC, P])

        pq = sb("pq", [P, H, H, HD])
        s1 = sb("s1", [P, H, H])
        mx1 = sb("mx1", [P, H])
        e1 = sb("e1", [P, H, H])
        rs1 = sb("rs1", [P, H])
        ri1 = sb("ri1", [P, H])
        pa = sb("pa", [P, H, HD, H])
        o1 = sb("o1", [P, H, HD])
        ctx1 = sb("ctx1", [P, HD, 32])
        y1 = sb("y1", [P, 2, 160])
        y2 = sb("y2", [P, 5, 64])

        bank_a = pb("bank_a")
        bank_s = ctx.enter_context(nc.psum_tensor("bank_s", [P, 2, 512], F32))
        bank_b = pb("bank_b")
        bank_c = pb("bank_c")
        bank_e = pb("bank_e")
        bank_f = pb("bank_f")
        bank_g = pb("bank_g")

        load = {n: sem("load_" + n) for n in (
            "c", "kmask", "wa0", "ba0", "wa1", "x0", "x", "qk", "v", "p0", "up0", "dn0", "qkv1", "wp1", "up1", "dn1")}
        S = {}
        for n in (
                "cleared built ones act_c dve_c1 dve_c2 dve_c pe_cT act_cT pe_mod0 pe_mod1 pe_mod2 pe_mod3 "
                "act_mod0 act_mod1 act_mod2 act_mod3 split0 split1 rest_ones rest middle warm borders zeros_qkv zeros_behind zeros_up padded w2half "
                "zeroed held "
                "pe_rep0 pe_rep1 pe_rep2 pe_rep3 act_rep0 act_rep1 act_rep2 act_rep3 "
                "stats0 stats1 stats2 stats3 var0 var1 var2 var3 pool_ve0 pool_ve1 pool_ve2 pool_ve3 "
                "rstd0 rstd1 rstd2 rstd3 cen0 cen1 cen2 cen3 xm0 xm1 xm2 xm3 "
                "pe_xT0 pe_xT1 pe_xT2 pe_xT3 act_xT0 act_xT1 act_xT2 act_xT3 "
                "pe_v act_v pe_qk act_q act_k pe_s dve_mx dve_s act_p "
                "pe_pT act_pT pe_av dve_rs dve_ctx pe_cxT act_cxT pe_pr0 dve_g0 dve_x0 "
                "pe_up0 act_th dve_h pe_dn0 dve_g1 dve_x1 "
                "pe_qkv act_qkv dve_mx1 dve_e1 act_p1 dve_sum1 dve_ri1 dve_ctx1 dve_y1 dve_y2 pe_pr1 dve_g2 dve_x2 "
                "pe_up1 act_h1 pe_dn1 dve_g3 dve_x3 out "
                "pool_pq dve_pq dve_s1 pool_pa dve_pa dve_o1").split():
            S[n] = sem(n)

        def tile(ap, t):
            return ap[:, bass.ds(t, 1), :].rearrange("p a f -> p (a f)")

        def mod(t, k):
            return MOD[:, bass.ds(t, 1), k, :].rearrange("p a f -> p (a f)")

        def row(ap):
            return ap.rearrange("(a n) -> a n", a=1)

        def chunks(ap, p):
            return ap.rearrange("(k p) n -> p k n", p=p)

        def head_scores(engine, t, piece):
            hs = slice(piece * HG, (piece + 1) * HG)
            q = tile(QKV, t)[:, 0:D].rearrange("p (h d) -> p h d", d=HD)[:, hs, :]
            k = tile(QKV, t)[:, D:2 * D].rearrange("p (h d) -> p h d", d=HD)
            return engine.tensor_tensor(pq[:, hs], q.unsqueeze(2).broadcast_to([P, HG, H, HD]),
                                        k.unsqueeze(1).broadcast_to([P, HG, H, HD]), ALU.mult)

        def head_values(engine, t, piece):
            hs = slice(piece * HG, (piece + 1) * HG)
            p = tile(P1, t).rearrange("p (h k) -> p h k", k=H)[:, hs, :]
            v = tile(QKV, t)[:, 2 * D:3 * D].rearrange("p (h d) -> p d h", d=HD)
            return engine.tensor_tensor(pa[:, hs], p.unsqueeze(2).broadcast_to([P, HG, HD, H]),
                                        v.unsqueeze(1).broadcast_to([P, HG, HD, H]), ALU.mult)

        def first(t):
            return isinstance(t, int) and t == 0

        def hold_wait(engine, t):
            if not isinstance(t, int):
                engine.sem_inc(S["held"], 1)

        def pipeline(engine, turn):
            for i in range(LOOP_FROM):
                turn(i, lambda lag, i=i: 0 <= i - lag < TILES)
            with engine.Fori(LOOP_FROM, TILES) as i:
                turn(i, lambda lag: True)
            for i in range(TILES, TILES + MAX_LAG):
                turn(i, lambda lag, i=i: 0 <= i - lag < TILES)

        def load_weights(engine, dst, src, bias, done, zeros):
            engine.dma_start(dst[1:P, 0, :], src[0:P - 1, :]).then_inc(load[done], 16)
            if bias is not None:
                engine.dma_start(dst[0:1, 0, :], row(bias)).then_inc(load[done], 16)
            engine.wait_ge(S[zeros[0]], zeros[1])
            engine.dma_start(dst[0:REST, 1, :], src[P - 1:D, :]).then_inc(load[done], 16)

        block = ctx.enter_context(nc.Block())

        @block.sync
        def _(sp):
            x_t = x.rearrange("b s f -> (b s) f").rearrange("(t p) f -> p t f", p=P)
            out_t = out.rearrange("b s f -> (b s) f").rearrange("(t p) f -> p t f", p=P)

            def load_w2(i, weights, bias):
                full = (MC - 1) * P
                sp.dma_start(w2[i][:, 0:MC - 1, :], chunks(weights[0:full], P)).then_inc(load[f"dn{i}"], 16)
                sp.dma_start(w2[i][0:ML, MC - 1, :], weights[full:MLP]).then_inc(load[f"dn{i}"], 16)
                sp.dma_start(w2[i][ML:ML + 1, MC - 1, :], row(bias)).then_inc(load[f"dn{i}"], 16)

            sp.dma_start(cnd[:], cond).then_inc(load["c"], 16)
            sp.dma_start(wa[0][0:KP], chunks(w["L0_cond_Wa"], KP)).then_inc(load["wa0"], 16)
            sp.dma_start(X[:, 0, :], x_t[:, 0, :]).then_inc(load["x0"], 16)
            load_weights(sp, wqk0[:, :, 0, :], w["L0_cond_Wq"], None, "qk", ("zeros_qkv", 1))
            load_weights(sp, wqk0[:, :, 1, :], w["L0_cond_Wk"], None, "qk", ("zeros_qkv", 1))
            load_weights(sp, wv, w["L0_cond_Wv"], None, "v", ("zeros_qkv", 1))
            sp.dma_start(X[:, 1:TILES, :], x_t[:, 1:TILES, :]).then_inc(load["x"], 16)
            load_weights(sp, wp0, w["L0_cond_Wp"], w["L0_cond_bp"], "p0", ("zeros_behind", 1))
            load_weights(sp, w1[0], w["L0_cond_W1"], w["L0_cond_b1"], "up0", ("zeros_up", 1))
            load_w2(0, w["L0_cond_W2"], w["L0_cond_b2"])
            load_weights(sp, wqkv, w["L1_cond_qkv_w"], w["L1_cond_qkv_b"], "qkv1", ("zeros_behind", 1))
            by_d = w["L1_cond_proj_w"].rearrange("(l d) n -> l d n", d=HD)
            for s in range(SEQS):
                for odd in range(2):
                    at = 32 * s + 16 * odd
                    sp.dma_start(wp1[at:at + 16, 0:5 - odd, :], by_d[:, odd:HD:2, :]).then_inc(load["wp1"], 16)
                sp.dma_start(wp1[32 * s + 16:32 * s + 17, 4, :], row(w["L1_cond_proj_b"])).then_inc(load["wp1"], 16)
            load_weights(sp, w1[1], w["L1_cond_fc1_w"], w["L1_cond_fc1_b"], "up1", ("zeros_up", 2))
            load_w2(1, w["L1_cond_fc2_w"], w["L1_cond_fc2_b"])

            with sp.Fori(0, TILES) as t:
                sp.wait_ge(S["dve_x3"], t + 1)
                sp.dma_start(out_t[:, bass.ds(t, 1), :], X[:, bass.ds(t, 1), :]).then_inc(S["out"], 16)
            sp.wait_ge(S["out"], 16 * TILES)

        @block.gpsimd
        def _(pool):
            nc.gpsimd.memset(ident[:], 0.0).then_inc(S["cleared"], 1)
            nc.gpsimd.memset(tileb[:], 0.0).then_inc(S["cleared"], 1)
            nc.gpsimd.memset(selb[:], 0.0).then_inc(S["cleared"], 1)
            nc.gpsimd.memset(causalb[:], 0.0).then_inc(S["cleared"], 1)
            for i in LN:
                nc.gpsimd.memset(xm[i][:, 0:1], 1.0)
                nc.gpsimd.memset(xm[i][:, 1 + D:KC * P], 0.0)
            nc.gpsimd.memset(ctx0[:, 0:1], 1.0)
            nc.gpsimd.memset(ctx0[:, 1 + D:KC * P], 0.0).then_inc(S["borders"], 1)
            pool.wait_ge(S["cleared"], 4)

            def fill(ap, keep, value, base, pattern):
                return nc.gpsimd.affine_select(out=ap, in_=ap, compare_op=keep, fill=value, base=base,
                                               pattern=pattern, channel_multiplier=1)

            fill(ident[:], ALU.not_equal, 1.0, 0, [[-1, P]]).then_inc(S["built"], 1)
            for s in range(3):
                fill(tileb[:], ALU.not_equal, 1.0, -32 * s, [[-SEQS, TILES], [-1, SEQS], [0, SEQ]]).then_inc(S["built"], 1)
                pool.wait_ge(S["built"], s + 2)
            nc.gpsimd.memset(wp0[:, 1, :], 0.0)
            nc.gpsimd.memset(wqkv[:, 1, :], 0.0).then_inc(S["zeros_behind"], 1)
            nc.gpsimd.memset(w1[0][:, 1, :], 0.0).then_inc(S["zeros_up"], 1)
            nc.gpsimd.memset(w1[1][:, 1, :], 0.0).then_inc(S["zeros_up"], 1)
            fill(selb[:], ALU.not_equal, 1.0, 0, [[0, SEQS], [-1, SEQ]]).then_inc(S["built"], 1)
            fill(causalb[:], ALU.is_ge, MASKED, 0, [[0, 8], [-1, SEQ]]).then_inc(S["built"], 1)

            def rest_of_setup():
                for ap in (ctx1, y1):
                    last = nc.gpsimd.memset(ap[:], 0.0)
                last.then_inc(S["cleared"], 1)
                pool.wait_ge(S["cleared"], 5)
                nc.gpsimd.memset(hT[0][ML:ML + 1, MC - 1, :], 1.0)
                nc.gpsimd.memset(hT[1][ML:ML + 1, MC - 1, :], 1.0).then_inc(S["cleared"], 1)
                pool.wait_ge(S["cleared"], 6)
                nc.gpsimd.memset(y1[:, :, D:D + 1], 1.0).then_inc(S["rest_ones"], 1)

            def inverse_root(t, i):
                pool.wait_ge(S[f"var{i}"], t + 1)
                nc.gpsimd.tensor_tensor(ve[i][:], mv[i][:, 1:2], epst[:], ALU.add).then_inc(S[f"pool_ve{i}"], 1)
                pool.wait_ge(S[f"pool_ve{i}"], t + 1)
                nc.gpsimd.tensor_tensor(rstd[i][:], ve[i][:], mhalf[:], ALU.pow).then_inc(S[f"rstd{i}"], 1)

            def score_products(t, piece):
                if not first(t):
                    pool.wait_ge(S["dve_s1"], t * HG)
                pool.wait_ge(S["act_qkv"], t + 1)
                head_scores(nc.gpsimd, t, piece).then_inc(S["pool_pq"], 1)

            def value_products(t, piece):
                if not first(t):
                    pool.wait_ge(S["dve_o1"], t * HG)
                pool.wait_ge(S["act_p1"], t + 1)
                head_values(nc.gpsimd, t, piece).then_inc(S["pool_pa"], 1)

            def turn(i, have):
                if have(5):
                    t = i - 5
                    value_products(t, 1)
                if have(1):
                    t = i - 1
                    inverse_root(t, 0)
                if isinstance(i, int) and i == 0:
                    rest_of_setup()
                if have(3):
                    t = i - 3
                    inverse_root(t, 1)
                if have(5):
                    t = i - 5
                    value_products(t, 2)
                if have(4):
                    t = i - 4
                    score_products(t, 0)
                    score_products(t, 1)
                    score_products(t, 2)
                if have(3):
                    t = i - 3
                    inverse_root(t, 2)
                if have(4):
                    t = i - 4
                    value_products(t, 0)
                if have(5):
                    t = i - 5
                    inverse_root(t, 3)
            pipeline(pool, turn)

        @block.scalar
        def _(act):
            act.dma_start(wa[0][KP:KP + 1, 0, :], row(w["L0_cond_ba"])).then_inc(load["ba0"], 16)
            act.dma_start(wa[0][KP:KP + 1, 1, :], ones_of_scales).then_inc(load["ba0"], 16)
            act.wait_ge(load["c"], 16)
            nc.scalar.activation(cth[:], cnd[:], ACT.Tanh, scale=0.5).then_inc(S["act_c"], 1)
            act.dma_start(wa[1][0:KP], chunks(w["L1_cond_ada_w"], KP)).then_inc(load["wa1"], 16)
            act.dma_start(wa[1][KP:KP + 1, 0, :], row(w["L1_cond_ada_b"])).then_inc(load["wa1"], 16)
            act.dma_start(wa[1][KP:KP + 1, 1, :], ones_of_scales).then_inc(load["wa1"], 16)
            act.wait_ge(S["pe_cT"], 1)
            act.wait_ge(S["ones"], 1)
            nc.scalar.activation(cT[0:KP], bank_a[0:KP, 0:KC * NSEQ].rearrange("p (k b) -> p k b", k=KC).unsqueeze(2)
                                 .broadcast_to([KP, KC, 3, NSEQ]), ACT.Copy).then_inc(S["act_cT"], 1)
            act.dma_start(kmask[:], heads).then_inc(load["kmask"], 16)

            def modulation(q):
                act.wait_ge(S[f"pe_mod{q}"], 1)
                nc.scalar.activation(stack[q // 2][:, q % 2 * 3 * D:(q % 2 + 1) * 3 * D],
                                     (bank_b, bank_c, bank_f, bank_g)[q][0:96, 0:3 * D], ACT.Copy
                                     ).then_inc(S[f"act_mod{q}"], 1)

            modulation(0)
            modulation(1)

            def copy_replicated(t, q):
                act.wait_ge(S[f"pe_rep{q}"], t + 1)
                nc.scalar.activation(MOD[:, bass.ds(t, 1), 3 * q:3 * q + 3, :].rearrange("p a k f -> p (a k f)"),
                                     bank_e[:, 0:3 * D], ACT.Copy).then_inc(S[f"act_rep{q}"], 1)

            def copy_norm(t, i):
                ps = (bank_a, bank_b, bank_e, bank_f)[i]
                act.wait_ge(S[f"pe_xT{i}"], t + 1)
                nc.scalar.activation(xmT[i][:].rearrange("p k t -> p (k t)"), ps[:, 0:KC * P], ACT.Copy
                                     ).then_inc(S[f"act_xT{i}"], 1)

            def spread_values(t):
                if first(t):
                    act.wait_ge(S["ones"], 2)
                if not first(t):
                    act.wait_ge(S["pe_av"], t)
                act.wait_ge(S["pe_v"], t + 1)
                for h in range(HG):
                    r = slice(32 * h, 32 * h + 32)
                    last = nc.scalar.activation(Vx[r, :, :, h, 0:HD].rearrange("p b g d -> p (b g) d"),
                                                bank_s[r, 0, 0:D].rearrange("p (a d) -> p a d", d=HD), ACT.Copy)
                last.then_inc(S["act_v"], 1)

            def copy_queries(t):
                act.wait_ge(S["pe_qk"], t + 1)
                nc.scalar.activation(qT[:].rearrange("p j t -> p (j t)"), bank_a[0:HI + GW, 0:2 * P], ACT.Copy
                                     ).then_inc(S["act_q"], 1)

            def spread_keys(t):
                if first(t):
                    act.wait_ge(load["kmask"], 16)
                act.wait_ge(S["pe_qk"], t + 1)
                for h in range(HG):
                    last = nc.scalar.activation(
                        Kx[:, :, :, h, :].rearrange("p j b k -> p (j b) k"),
                        bank_a[0:HI + GW, 2 * P:4 * P].rearrange("p (a k) -> p a k", k=SEQ), ACT.Copy,
                        scale=kmask[:, h:h + 1])
                last.then_inc(S["act_k"], 1)

            def exp_causal(t):
                act.wait_ge(S["dve_s"], t + 1)
                nc.scalar.activation(p0[:], s0[:], ACT.Exp, scale=SCALE).then_inc(S["act_p"], 1)

            def copy_probs(t):
                act.wait_ge(S["pe_pT"], t + 1)
                nc.scalar.activation(pT[:].rearrange("p g t -> p (g t)"), bank_b[:], ACT.Copy).then_inc(S["act_pT"], 1)

            def copy_context(t):
                act.wait_ge(S["pe_cxT"], t + 1)
                nc.scalar.activation(ctxT[:].rearrange("p k t -> p (k t)"), bank_b[:, 0:KC * P], ACT.Copy
                                     ).then_inc(S["act_cxT"], 1)

            def tanh_hidden(t):
                act.wait_ge(S["pe_up0"], t + 1)
                nc.scalar.activation(th[:, 0:MC - 1, :].rearrange("p m t -> p (m t)"), bank_b[:], ACT.Tanh, scale=0.5)
                nc.scalar.activation(th[0:ML, MC - 1, :], bank_c[0:ML, 0:P], ACT.Tanh, scale=0.5).then_inc(S["act_th"], 1)

            def copy_qkv(t):
                act.wait_ge(S["pe_qkv"], t + 1)
                nc.scalar.activation(tile(QKV, t), bank_e[:, 0:3 * D], ACT.Copy).then_inc(S["act_qkv"], 1)

            def exp_heads(t):
                act.wait_ge(S["dve_e1"], t + 1)
                nc.scalar.activation(tile(P1, t), e1[:].rearrange("p h k -> p (h k)"), ACT.Exp, scale=SCALE
                                     ).then_inc(S["act_p1"], 1)

            def gelu_hidden(t):
                act.wait_ge(S["pe_up1"], t + 1)
                nc.scalar.activation(hT[1][:, 0:MC - 1, :].rearrange("p m t -> p (m t)"), bank_f[:], ACT.Gelu)
                nc.scalar.activation(hT[1][0:ML, MC - 1, :], bank_g[0:ML, 0:P], ACT.Gelu).then_inc(S["act_h1"], 1)

            def turn(i, have):
                if have(2):
                    t = i - 2
                    exp_causal(t)
                if have(0):
                    t = i
                    copy_replicated(t, 0)
                if isinstance(i, int) and i == 0:
                    modulation(2)
                    modulation(3)
                if have(1):
                    t = i - 1
                    copy_queries(t)
                if have(2):
                    t = i - 2
                    copy_probs(t)
                if have(1):
                    t = i - 1
                    spread_keys(t)
                if have(0):
                    t = i
                    copy_replicated(t, 1)
                if have(4):
                    t = i - 4
                    exp_heads(t)
                if have(2):
                    t = i - 2
                    copy_replicated(t, 3)
                    copy_context(t)
                if have(3):
                    t = i - 3
                    copy_norm(t, 2)
                if have(1):
                    t = i - 1
                    spread_values(t)
                if have(5):
                    t = i - 5
                    copy_norm(t, 3)
                if have(3):
                    t = i - 3
                    copy_qkv(t)
                if have(1):
                    t = i - 1
                    copy_replicated(t, 2)
                if have(2):
                    t = i - 2
                    copy_norm(t, 1)
                if have(0):
                    t = i
                    copy_norm(t, 0)
                if have(5):
                    t = i - 5
                    gelu_hidden(t)
                if have(2):
                    t = i - 2
                    tanh_hidden(t)
            pipeline(act, turn)

        @block.vector
        def _(dve):
            nc.vector.memset(warm[:], 0.0).then_inc(S["warm"], 1)
            nc.vector.memset(wqk0[:, 1, :, :], 0.0)
            nc.vector.memset(wqk0[0:1, 0, :, :], 0.0)
            nc.vector.memset(wv[0:1, 0, :], 0.0)
            nc.vector.memset(wv[:, 1, :], 0.0).then_inc(S["zeros_qkv"], 1)
            nc.vector.memset(cT[:], 1.0).then_inc(S["ones"], 1)
            nc.vector.memset(epst[:], EPS)
            nc.vector.memset(mhalf[:], -0.5)
            nc.vector.memset(wqk[:], 0.0).then_inc(S["zeroed"], 1)
            dve.wait_ge(S["act_c"], 1)
            nc.vector.tensor_tensor(cgt[:], cth[:], cnd[:], ALU.mult).then_inc(S["dve_c1"], 1)
            dve.wait_ge(S["dve_c1"], 1)
            nc.vector.tensor_tensor(cth[:], cgt[:], cnd[:], ALU.add).then_inc(S["dve_c2"], 1)
            dve.wait_ge(S["dve_c2"], 1)
            nc.vector.tensor_scalar_mul(csl[:], cth[:], 0.5).then_inc(S["dve_c"], 1)
            nc.vector.memset(Vx[:], 0.0).then_inc(S["zeroed"], 1)
            dve.wait_ge(S["zeroed"], 2)
            for h in range(HG):
                last = nc.vector.memset(Vx[32 * h:32 * h + 32, :, :, h, HD:HD + 1], 1.0)
            last.then_inc(S["ones"], 1)
            dve.wait_ge(load["qk"], 4 * 16)
            for which in range(2):
                for r, at in enumerate((LO, HI)):
                    last = nc.vector.tensor_copy(wqk[:, :, which, :, at:at + GW],
                                                 wqk0[:, :, which, :].rearrange("p k (j r c) -> p k j r c", j=2, r=2)[:, :, :, r, :])
            last.then_inc(S["padded"], 1)

            def split_modulation(q):
                low = slice(64, 96)
                high = stack[q // 2][:, q % 2 * 3 * D:(q % 2 + 1) * 3 * D]
                if q:
                    dve.wait_ge(S[f"split{(q - 1) // 2}"], (q - 1) % 2 + 1)
                dve.wait_ge(S[f"act_mod{q}"], 1)
                nc.vector.tensor_tensor(rest[:], (bank_b, bank_c, bank_f, bank_g)[q][0:96, 0:3 * D], high, ALU.subtract
                                        ).then_inc(S["rest"], 1)
                dve.wait_ge(S["rest"], q + 1)
                nc.vector.tensor_copy(midb[low], rest[low]).then_inc(S["middle"], 1)
                nc.vector.tensor_copy(high[32:64], rest[32:64])
                dve.wait_ge(S["middle"], q + 1)
                nc.vector.tensor_tensor(high[low], rest[low], midb[low], ALU.subtract).then_inc(S[f"split{q // 2}"], 1)

            split_modulation(0)

            def halve_w2():
                dve.wait_ge(load["dn0"], 3 * 16)
                nc.vector.tensor_scalar_mul(w2[0][:, 0:MC - 1, :], w2[0][:, 0:MC - 1, :], 0.5)
                nc.vector.tensor_scalar_mul(w2[0][0:ML, MC - 1, :], w2[0][0:ML, MC - 1, :], 0.5).then_inc(S["w2half"], 1)

            def statistics(t, i):
                if isinstance(t, int) and i == 0 and t < 2:
                    dve.wait_ge(load[("x0", "x")[t]], 16)
                    hold_wait(dve, t)
                if i:
                    dve.wait_ge(S[f"dve_x{i - 1}"], t + 1)
                    hold_wait(dve, t)
                nc.vector.bn_stats(st[i][:], tile(X, t)).then_inc(S[f"stats{i}"], 1)

            def variance(t, i):
                dve.wait_ge(S[f"stats{i}"], t + 1)
                hold_wait(dve, t)
                nc.vector.bn_aggr(mv[i][:], st[i][:]).then_inc(S[f"var{i}"], 1)

            def centre(t, i):
                q = i
                dve.wait_ge(S[f"act_rep{q}"], t + 1)
                dve.wait_ge(S[f"var{i}"], t + 1)
                nc.vector.scalar_tensor_tensor(u[i][:], tile(X, t), mv[i][:, 0:1], mod(t, 3 * i + 1), ALU.subtract, ALU.mult
                                               ).then_inc(S[f"cen{i}"], 1)

            def modulate(t, i):
                dve.wait_ge(S[f"rstd{i}"], t + 1)
                dve.wait_ge(S[f"cen{i}"], t + 1)
                nc.vector.scalar_tensor_tensor(xm[i][:, 1:1 + D], u[i][:], rstd[i][:], mod(t, 3 * i), ALU.mult, ALU.add
                                               ).then_inc(S[f"xm{i}"], 1)

            def gate(t, i):
                done = ("pe_pr0", "pe_dn0", "pe_pr1", "pe_dn1")[i]
                ps = (bank_c, bank_e, bank_g, bank_g)[i]
                at = 2 * P if i == 3 else 0
                if i == 3 and not first(t):
                    dve.wait_ge(S["dve_x3"], t)
                dve.wait_ge(S[done], t + 1)
                nc.vector.tensor_tensor(g[i][:], ps[:, at:at + D], mod(t, 3 * i + 2), ALU.mult).then_inc(S[f"dve_g{i}"], 1)

            def residual(t, i):
                dve.wait_ge(S[f"dve_g{i}"], t + 1)
                nc.vector.tensor_tensor(tile(X, t), tile(X, t), g[i][:], ALU.add).then_inc(S[f"dve_x{i}"], 1)

            scores = bank_s[:, :, 0:8 * SEQ].rearrange("p r (h k) -> p r h k", k=SEQ)

            def causal_max(t):
                dve.wait_ge(S["pe_s"], t + 1)
                nc.vector.tensor_reduce(mx0[:], scores, axis=AX.X, op=ALU.max).then_inc(S["dve_mx"], 1)

            def causal_shift(t):
                dve.wait_ge(S["dve_mx"], t + 1)
                nc.vector.tensor_tensor(s0[:], scores, mx0[:].unsqueeze(3).broadcast_to([P, 2, 8, SEQ]), ALU.subtract
                                        ).then_inc(S["dve_s"], 1)

            weighted = bank_c[:, 0:H * (HD + 1)].rearrange("p (h e) -> p h e", e=HD + 1)

            def causal_sum_inverse(t):
                dve.wait_ge(S["pe_av"], t + 1)
                nc.vector.reciprocal(rs0[:].unsqueeze(2), weighted[:, :, HD:HD + 1]).then_inc(S["dve_rs"], 1)

            def causal_context(t):
                dve.wait_ge(S["dve_rs"], t + 1)
                nc.vector.tensor_tensor(ctx0[:, 1:1 + D].rearrange("p (h d) -> p h d", d=HD), weighted[:, :, 0:HD],
                                        rs0[:].unsqueeze(2).broadcast_to([P, H, HD]), ALU.mult).then_inc(S["dve_ctx"], 1)

            def silu_hidden(t):
                dve.wait_ge(S["act_th"], t + 1)
                nc.vector.scalar_tensor_tensor(hT[0][:, 0:MC - 1, :].rearrange("p m t -> p (m t)"),
                                               th[:, 0:MC - 1, :].rearrange("p m t -> p (m t)"), 1.0, bank_b[:],
                                               ALU.add, ALU.mult)
                nc.vector.scalar_tensor_tensor(hT[0][0:ML, MC - 1, :], th[0:ML, MC - 1, :], 1.0, bank_c[0:ML, 0:P],
                                               ALU.add, ALU.mult).then_inc(S["dve_h"], 1)

            def score_products(t, piece):
                dve.wait_ge(S["act_qkv"], t + 1)
                head_scores(nc.vector, t, piece).then_inc(S["dve_pq"], 1)

            def value_products(t, piece):
                dve.wait_ge(S["act_p1"], t + 1)
                head_values(nc.vector, t, piece).then_inc(S["dve_pa"], 1)

            def sum_scores(t, piece):
                hs = slice(piece * HG, (piece + 1) * HG)
                if piece < POOL_PIECES:
                    dve.wait_ge(S["pool_pq"], t * POOL_PIECES + piece + 1)
                else:
                    dve.wait_ge(S["dve_pq"], t + 1)
                nc.vector.tensor_reduce(s1[:, hs], pq[:, hs], axis=AX.X, op=ALU.add).then_inc(S["dve_s1"], 1)

            def heads_max(t):
                dve.wait_ge(S["dve_s1"], t * HG + HG)
                nc.vector.tensor_reduce(mx1[:], s1[:], axis=AX.X, op=ALU.max).then_inc(S["dve_mx1"], 1)

            def heads_shift(t):
                dve.wait_ge(S["dve_mx1"], t + 1)
                nc.vector.tensor_tensor(e1[:], s1[:], mx1[:].unsqueeze(2).broadcast_to([P, H, H]), ALU.subtract
                                        ).then_inc(S["dve_e1"], 1)

            def heads_sum(t):
                dve.wait_ge(S["act_p1"], t + 1)
                nc.vector.tensor_reduce(rs1[:], tile(P1, t).rearrange("p (h k) -> p h k", k=H), axis=AX.X, op=ALU.add
                                        ).then_inc(S["dve_sum1"], 1)

            def heads_sum_inverse(t):
                dve.wait_ge(S["dve_sum1"], t + 1)
                nc.vector.reciprocal(ri1[:], rs1[:]).then_inc(S["dve_ri1"], 1)

            def sum_values(t, piece):
                hs = slice(piece * HG, (piece + 1) * HG)
                if piece < POOL_PIECES:
                    dve.wait_ge(S["pool_pa"], t * POOL_PIECES + piece + 1)
                else:
                    dve.wait_ge(S["dve_pa"], t + 1)
                nc.vector.tensor_reduce(o1[:, hs], pa[:, hs], axis=AX.X, op=ALU.add).then_inc(S["dve_o1"], 1)

            def heads_context(t):
                dve.wait_ge(S["dve_ri1"], t + 1)
                dve.wait_ge(S["dve_o1"], t * HG + HG)
                nc.vector.tensor_tensor(ctx1[:, :, 0:H].rearrange("p d h -> p h d"), o1[:],
                                        ri1[:].unsqueeze(2).broadcast_to([P, H, HD]), ALU.mult).then_inc(S["dve_ctx1"], 1)

            def heads_to_rows(t):
                dve.wait_ge(S["dve_ctx1"], t + 1)
                nc.vector.transpose(y1[:, :, 0:D].rearrange("p a (d l) -> p d a l", l=16), ctx1[:]).then_inc(S["dve_y1"], 1)

            def features_to_rows(t):
                dve.wait_ge(S["dve_y1"], t + 1)
                nc.vector.transpose(y2[:].rearrange("p j (c a) -> p a j c", a=2),
                                    y1[:].rearrange("p a (j x) -> p a j x", x=32)).then_inc(S["dve_y2"], 1)

            def turn(i, have):
                if have(0):
                    t = i
                    statistics(t, 0)
                if have(5):
                    t = i - 5
                    statistics(t, 3)
                    variance(t, 3)
                if have(0):
                    t = i
                    variance(t, 0)
                if isinstance(i, int) and i == 0:
                    split_modulation(1)
                if have(4):
                    t = i - 4
                    heads_sum(t)
                if have(5):
                    t = i - 5
                    centre(t, 3)
                if have(0):
                    t = i
                    centre(t, 0)
                if have(2):
                    t = i - 2
                    gate(t, 0)
                    residual(t, 0)
                if have(5):
                    t = i - 5
                    modulate(t, 3)
                if have(2):
                    t = i - 2
                    statistics(t, 1)
                if have(4):
                    t = i - 4
                    heads_sum_inverse(t)
                    sum_values(t, 0)
                if have(2):
                    t = i - 2
                    variance(t, 1)
                if have(4):
                    t = i - 4
                    value_products(t, 3)
                    sum_values(t, 1)
                if have(2):
                    t = i - 2
                    centre(t, 1)
                if have(0):
                    t = i
                    modulate(t, 0)
                if isinstance(i, int) and i == 0:
                    split_modulation(2)
                    split_modulation(3)
                    halve_w2()
                if have(2):
                    t = i - 2
                    modulate(t, 1)
                if have(4):
                    t = i - 4
                    sum_values(t, 3)
                    sum_values(t, 2)
                if have(3):
                    t = i - 3
                    score_products(t, 3)
                if have(1):
                    t = i - 1
                    causal_max(t)
                if have(3):
                    t = i - 3
                    sum_scores(t, 3)
                if have(1):
                    t = i - 1
                    causal_shift(t)
                if have(4):
                    t = i - 4
                    heads_context(t)
                if have(3):
                    t = i - 3
                    sum_scores(t, 0)
                if have(4):
                    t = i - 4
                    heads_to_rows(t)
                if have(3):
                    t = i - 3
                    sum_scores(t, 1)
                if have(2):
                    t = i - 2
                    silu_hidden(t)
                if have(3):
                    t = i - 3
                    sum_scores(t, 2)
                if have(4):
                    t = i - 4
                    features_to_rows(t)
                if have(3):
                    t = i - 3
                    heads_max(t)
                if have(5):
                    t = i - 5
                    gate(t, 3)
                if have(2):
                    t = i - 2
                    gate(t, 1)
                    residual(t, 1)
                if have(1):
                    t = i - 1
                    causal_sum_inverse(t)
                if have(2):
                    t = i - 2
                    statistics(t, 2)
                if have(1):
                    t = i - 1
                    causal_context(t)
                if have(2):
                    t = i - 2
                    variance(t, 2)
                if have(3):
                    t = i - 3
                    heads_shift(t)
                if have(5):
                    t = i - 5
                    residual(t, 3)
                if have(2):
                    t = i - 2
                    centre(t, 2)
                if have(4):
                    t = i - 4
                    gate(t, 2)
                if have(2):
                    t = i - 2
                    modulate(t, 2)
                if have(4):
                    t = i - 4
                    residual(t, 2)

            pipeline(dve, turn)

        @block.tensor
        def _(pe):
            mm = nc.tensor.matmul
            pe.wait_ge(S["warm"], 1)
            for k in range(WARMUP):
                mm(bank_g[:], warm[:, 0:P], warm[:], start=True, stop=True)
            pe.wait_ge(S["built"], 1)
            pe.wait_ge(S["dve_c"], 1)
            for k in range(KC):
                last = nc.tensor.transpose(bank_a[0:KP, k * NSEQ:(k + 1) * NSEQ], csl[:, k * KP:(k + 1) * KP],
                                           ident[0:NSEQ, 0:NSEQ])
            last.then_inc(S["pe_cT"], 1)
            pe.wait_ge(S["act_cT"], 1)

            def modulation(q):
                for k in range(KC):
                    last = mm((bank_b, bank_c, bank_f, bank_g)[q][0:96, 0:3 * D], cT[:, k, :],
                              wa[q // 2][:, k, q % 2 * 3 * D:(q % 2 + 1) * 3 * D], start=k == 0, stop=k == KC - 1)
                last.then_inc(S[f"pe_mod{q}"], 1)

            pe.wait_ge(load["wa0"], 16)
            pe.wait_ge(load["ba0"], 2 * 16)
            modulation(0)
            modulation(1)

            def after_bank_e(i, have, readers):
                for signal, lag in readers:
                    if have(lag):
                        pe.wait_ge(S[signal], i - lag + 1)
                        return

            def replicate(t, q):
                if first(t):
                    pe.wait_ge(S[f"split{q // 2}"], q % 2 + 1)
                    pe.wait_ge(S["built"], 4)
                mm(bank_e[:, 0:3 * D], tileb[:, bass.ds(t, 1)].rearrange("p a s q -> p (a s q)"),
                   stack[q // 2][:, q % 2 * 3 * D:(q % 2 + 1) * 3 * D], start=True, stop=True).then_inc(S[f"pe_rep{q}"], 1)

            def transpose_norm(t, i):
                ps = (bank_a, bank_b, bank_e, bank_f)[i]
                if i in (0, 3) and not first(t):
                    pe.wait_ge(S["act_k" if i == 0 else "act_h1"], t)
                if first(t):
                    pe.wait_ge(S["borders"], 1)
                pe.wait_ge(S[f"xm{i}"], t + 1)
                for k in range(KC):
                    last = nc.tensor.transpose(ps[:, k * P:(k + 1) * P], xm[i][:, k * P:(k + 1) * P], ident[:])
                last.then_inc(S[f"pe_xT{i}"], 1)

            def values(t):
                if first(t):
                    pe.wait_ge(load["v"], 2 * 16)
                if not first(t):
                    pe.wait_ge(S["dve_s"], t)
                pe.wait_ge(S["act_xT0"], t + 1)
                for b in range(SEQS):
                    for k in range(KC):
                        for h in range(HG):
                            last = mm(bank_s[32 * h:32 * h + 32, 0, b * GW:(b + 1) * GW],
                                      xmT[0][:, k, b * SEQ:(b + 1) * SEQ],
                                      wv[:, k, :].rearrange("p (g h d) -> p g h d", g=HG, h=HG)[:, :, h, :],
                                      start=k == 0, stop=k == KC - 1)
                last.then_inc(S["pe_v"], 1)

            def queries_keys(t):
                if first(t):
                    pe.wait_ge(S["padded"], 1)
                pe.wait_ge(S["act_xT0"], t + 1)
                for which in range(2):
                    for j in range(2):
                        col = (2 * which + j) * P
                        for k in range(KC):
                            last = mm(bank_a[0:HI + GW, col:col + P], wqk[:, k, which, j, :], xmT[0][:, k, :],
                                      start=k == 0, stop=k == KC - 1)
                last.then_inc(S["pe_qk"], 1)

            def causal_scores(t):
                if first(t):
                    pe.wait_ge(S["built"], 6)
                pe.wait_ge(S["act_v"], t + 1)
                pe.wait_ge(S["act_q"], t + 1)
                pe.wait_ge(S["act_k"], t + 1)
                for r in range(2):
                    mm(bank_s[:, r, 0:8 * SEQ], selb[:].rearrange("p s q -> p (s q)"),
                       causalb[:].rearrange("p h k -> p (h k)"), start=True, stop=False, skip_group_check=True)
                for j in range(2):
                    for b in range(SEQS):
                        for r, at in enumerate((LO, HI)):
                            last = mm(bank_s[32 * b:32 * b + 32, r, j * P:(j + 1) * P],
                                      qT[at:at + GW, j, b * SEQ:(b + 1) * SEQ],
                                      Kx[at:at + GW, j, b].rearrange("p h k -> p (h k)"),
                                      start=False, stop=True, skip_group_check=True)
                last.then_inc(S["pe_s"], 1)

            def transpose_probs(t):
                if not first(t):
                    pe.wait_ge(S["dve_h"], t)
                pe.wait_ge(S["act_p"], t + 1)
                for k in range(HG):
                    last = nc.tensor.transpose(bank_b[:, k * P:(k + 1) * P],
                                               p0[:, k // 2, k % 2 * HG:k % 2 * HG + HG, :].rearrange("p h k -> p (h k)"),
                                               ident[:])
                last.then_inc(S["pe_pT"], 1)

            def weigh_values(t):
                pe.wait_ge(S["act_pT"], t + 1)
                for k in range(HG):
                    group = k % 2 * 2 + k // 2
                    for b in range(SEQS):
                        last = mm(bank_c[32 * b:32 * b + 32, group * HG * (HD + 1):(group + 1) * HG * (HD + 1)],
                                  pT[:, k, b * SEQ:(b + 1) * SEQ], Vx[:, b, group].rearrange("p h e -> p (h e)"),
                                  start=True, stop=True)
                last.then_inc(S["pe_av"], 1)

            def transpose_context(t):
                pe.wait_ge(S["dve_ctx"], t + 1)
                for k in range(KC):
                    last = nc.tensor.transpose(bank_b[:, k * P:(k + 1) * P], ctx0[:, k * P:(k + 1) * P], ident[:])
                last.then_inc(S["pe_cxT"], 1)

            def project0(t):
                if first(t):
                    pe.wait_ge(load["p0"], 3 * 16)
                pe.wait_ge(S["act_cxT"], t + 1)
                for k in range(KC):
                    last = mm(bank_c[:, 0:D], ctxT[:, k, :], wp0[:, k, :], start=k == 0, stop=k == KC - 1)
                last.then_inc(S["pe_pr0"], 1)

            def hidden(t, i):
                if first(t):
                    pe.wait_ge(load[f"up{i}"], 3 * 16)
                xi, big, small = ((1, bank_b, bank_c), (3, bank_f, bank_g))[i]
                pe.wait_ge(S[f"act_xT{xi}"], t + 1)
                for m in range(MC):
                    cols = P if m < MC - 1 else ML
                    dst = big[:, m * P:(m + 1) * P] if m < MC - 1 else small[0:ML, 0:P]
                    for k in range(KC):
                        last = mm(dst, w1[i][:, k, m * P:m * P + cols], xmT[xi][:, k, :],
                                  start=k == 0, stop=k == KC - 1)
                last.then_inc(S[f"pe_up{i}"], 1)

            def mlp_out(t, i):
                if first(t):
                    pe.wait_ge(load[f"dn{i}"], 3 * 16)
                    if i == 0:
                        pe.wait_ge(S["w2half"], 1)
                dst = (bank_e[:, 0:D], bank_g[:, 2 * P:2 * P + D])[i]
                pe.wait_ge(S[("dve_h", "act_h1")[i]], t + 1)
                for m in range(MC):
                    r = P if m < MC - 1 else ML + 1
                    last = mm(dst, hT[i][0:r, m, :], w2[i][0:r, m, :], start=m == 0, stop=m == MC - 1)
                last.then_inc(S[f"pe_dn{i}"], 1)

            def qkv1(t):
                if first(t):
                    pe.wait_ge(load["qkv1"], 3 * 16)
                pe.wait_ge(S["act_xT2"], t + 1)
                for k in range(KC):
                    last = mm(bank_e[:, 0:3 * D], xmT[2][:, k, :], wqkv[:, k, :], start=k == 0, stop=k == KC - 1)
                last.then_inc(S["pe_qkv"], 1)

            def project1(t):
                if first(t):
                    pe.wait_ge(load["wp1"], 3 * SEQS * 16)
                if not first(t):
                    pe.wait_ge(S["dve_g3"], t)
                pe.wait_ge(S["dve_y2"], t + 1)
                hold_wait(pe, t)
                for j in range(5):
                    rows = 32 if j < 4 else 17
                    for s in range(SEQS):
                        last = mm(bank_g[32 * s:32 * s + 32, 0:D], y2[32 * s:32 * s + rows, j, 0:SEQ],
                                  wp1[32 * s:32 * s + rows, j, :], start=j == 0, stop=j == 4)
                last.then_inc(S["pe_pr1"], 1)

            def turn(i, have):
                if have(3):
                    t = i - 3
                    transpose_norm(t, 1)
                if have(1):
                    t = i - 1
                    transpose_norm(t, 0)
                if have(0):
                    t = i
                    after_bank_e(i, have, (("act_rep2", 2), ("act_qkv", 4), ("act_rep3", 3), ("act_rep1", 1), ("dve_g1", 4), ("act_rep0", 1)))
                    replicate(t, 0)
                if isinstance(i, int) and i == 0:
                    pe.wait_ge(load["wa1"], 3 * 16)
                    modulation(2)
                    modulation(3)
                if have(3):
                    t = i - 3
                    hidden(t, 0)
                if have(1):
                    t = i - 1
                    queries_keys(t)
                if have(6):
                    t = i - 6
                    mlp_out(t, 1)
                if have(2):
                    t = i - 2
                    transpose_probs(t)
                if have(3):
                    t = i - 3
                    after_bank_e(i, have, (("act_rep0", 0), ("act_rep2", 2), ("act_qkv", 4), ("act_rep3", 3), ("act_rep1", 1), ("dve_g1", 4)))
                    mlp_out(t, 0)
                if have(2):
                    t = i - 2
                    weigh_values(t)
                if have(0):
                    t = i
                    after_bank_e(i, have, (("dve_g1", 3), ("act_rep0", 0), ("act_rep2", 2), ("act_qkv", 4), ("act_rep3", 3), ("act_rep1", 1)))
                    replicate(t, 1)
                if have(5):
                    t = i - 5
                    project1(t)
                if have(2):
                    t = i - 2
                    after_bank_e(i, have, (("act_rep1", 0), ("dve_g1", 3), ("act_rep0", 0), ("act_rep2", 2), ("act_qkv", 4), ("act_rep3", 3)))
                    replicate(t, 3)
                    transpose_context(t)
                if have(1):
                    t = i - 1
                    values(t)
                if have(3):
                    t = i - 3
                    after_bank_e(i, have, (("act_rep3", 2), ("act_rep1", 0), ("dve_g1", 3), ("act_rep0", 0), ("act_rep2", 2), ("act_qkv", 4)))
                    transpose_norm(t, 2)
                if have(2):
                    t = i - 2
                    project0(t)
                if have(3):
                    t = i - 3
                    qkv1(t)
                if have(5):
                    t = i - 5
                    transpose_norm(t, 3)
                if have(1):
                    t = i - 1
                    causal_scores(t)
                    after_bank_e(i, have, (("act_qkv", 3), ("act_rep3", 2), ("act_rep1", 0), ("dve_g1", 3), ("act_rep0", 0), ("act_rep2", 2)))
                    replicate(t, 2)
                if have(5):
                    t = i - 5
                    hidden(t, 1)
            pipeline(pe, turn)


_W = ['L0_cond_Wq', 'L0_cond_Wk', 'L0_cond_Wv', 'L0_cond_Wp', 'L0_cond_bp', 'L0_cond_W1', 'L0_cond_b1', 'L0_cond_W2',
      'L0_cond_b2', 'L0_cond_Wa', 'L0_cond_ba', 'L1_cond_qkv_w', 'L1_cond_qkv_b', 'L1_cond_proj_w', 'L1_cond_proj_b',
      'L1_cond_fc1_w', 'L1_cond_fc1_b', 'L1_cond_fc2_w', 'L1_cond_fc2_b', 'L1_cond_ada_w', 'L1_cond_ada_b']


def kernel(**inputs):
    import numpy as _np
    import concourse.bacc as _bacc
    from concourse import mybir as _mybir
    from concourse.bass_utils import run_bass_kernel_spmd as _run

    nc = _bacc.Bacc("TRN2", target_bir_lowering=False, num_devices=1)
    arrays, aps = {}, {}
    for name in ['x', 'cond_1152', *_W]:
        a = _np.ascontiguousarray(inputs[name])
        arrays[f"in_{name}"] = a
        aps[name] = nc.dram_tensor(f"in_{name}", a.shape, _mybir.dt.from_np(a.dtype), kind="ExternalInput").ap()
    arrays["in_head_rows"] = head_rows()
    heads = nc.dram_tensor("in_head_rows", (HI + GW, HG), F32, kind="ExternalInput").ap()
    out = nc.dram_tensor("out", (NSEQ, SEQ, D), F32, kind="ExternalOutput").ap()
    arrays["in_ones_of_scales"] = scale_ones()
    ones_of_scales = nc.dram_tensor("in_ones_of_scales", (1, NMOD * D), F32, kind="ExternalInput").ap()
    build(nc, aps["x"], aps["cond_1152"], {n: aps[n] for n in _W}, heads, ones_of_scales, out)
    r = _run(nc, [arrays], core_ids=[0])
    return r.results[0]["out"]
```
